# Optimizing a Trainium2 kernel written in Bass

```python
import numpy as np
import jax
import jax.numpy as jnp

def _softmax(x, axis=-1):
    return jax.nn.softmax(x, axis=axis)

def _gelu(x):
    return jax.nn.gelu(x, approximate=True)

def _silu(x):
    return jax.nn.silu(x)

def _sigmoid(x):
    return jax.nn.sigmoid(x)

def _layernorm(x, axis=-1, eps=1e-05):
    m = jnp.mean(x, axis=axis, keepdims=True)
    v = jnp.var(x, axis=axis, keepdims=True)
    return (x - m) / jnp.sqrt(v + eps)

def _scatter_add(tgt, idx, src, axis=0):
    return tgt.at[idx].add(src)

def _segment_sum(src, seg, n):
    return jax.ops.segment_sum(src, seg, n)
kernel_name = 'mk_macaron_d2_jaxref_r8_775653'

def setup_inputs(seed: int=0):
    np.random.seed(seed)
    _w = jnp.asarray

    def _L0_attn_setup():
        import jax, jax.numpy as jnp
        import numpy as np
        HEADS = 32
        DIM_HEAD = 32
        EPS = 1e-06
        key = jax.random.key(seed)
        k1, k2, k3 = jax.random.split(key, 3)
        b, n, dim = (2, 256, 128)
        x = jax.random.normal(k1, (b, n, dim), dtype=jnp.float32)
        w_qkv = jax.random.normal(k2, (dim, 3 * HEADS * DIM_HEAD), dtype=jnp.float32) * dim ** (-0.5)
        w_out = jax.random.normal(k3, (HEADS * DIM_HEAD, dim), dtype=jnp.float32) * dim ** (-0.5)
        b_out = jnp.zeros((dim,), dtype=jnp.float32)
        ln_gamma = jnp.ones((dim,), dtype=jnp.float32)
        ln_beta = jnp.zeros((dim,), dtype=jnp.float32)
        return {'x': x, 'w_qkv': w_qkv, 'w_out': w_out, 'b_out': b_out, 'ln_gamma': ln_gamma, 'ln_beta': ln_beta}
    _L0_attn_in = _L0_attn_setup()

    def _L0_ffn_setup():
        import jax, jax.numpy as jnp
        import numpy as np
        DIM = 128
        NUM_EXPERTS = 8
        TOP_K = 2
        HIDDEN = 4 * DIM // TOP_K
        BS, SLEN = (1, 256)

        def _moe(x, gate_w, w_up, w_down, expert_bias):
            bs, slen, dim = x.shape
            xf = x.reshape(-1, dim)
            scores = jax.nn.sigmoid(xf @ gate_w.T)
            biased = scores + expert_bias
            _, sel = jax.lax.top_k(biased, TOP_K)
            top_scores = jnp.take_along_axis(scores, sel, axis=-1)

            def body(acc, ew):
                e, wu, wd = ew
                w_t = jnp.sum(jnp.where(sel == e, top_scores, 0.0), axis=-1)
                xe = xf * w_t[:, None]
                h = jnp.square(jax.nn.relu(xe @ wu.T))
                return (acc + h @ wd.T, None)
            out0 = jnp.zeros_like(xf)
            out, _ = jax.lax.scan(body, out0, (jnp.arange(NUM_EXPERTS), w_up, w_down))
            return out.reshape(bs, slen, dim)
        key = jax.random.key(seed)
        k0, k1, k2, k3 = jax.random.split(key, 4)
        x = jax.random.normal(k0, (BS, SLEN, DIM), dtype=jnp.float32)
        gate_w = jax.random.normal(k1, (NUM_EXPERTS, DIM), dtype=jnp.float32) * 0.02
        w_up = jax.random.normal(k2, (NUM_EXPERTS, HIDDEN, DIM), dtype=jnp.float32) * 0.02
        w_down = jax.random.normal(k3, (NUM_EXPERTS, DIM, HIDDEN), dtype=jnp.float32) * 0.02
        expert_bias = jnp.zeros((NUM_EXPERTS,), dtype=jnp.float32)
        return {'x': x, 'gate_w': gate_w, 'w_up': w_up, 'w_down': w_down, 'expert_bias': expert_bias}
    _L0_ffn_in = _L0_ffn_setup()

    def _L1_attn_setup():
        import jax, jax.numpy as jnp
        import numpy as np
        N, L, D_IN, H, HD, D_OUT = (4, 256, 128, 16, 64, 128)
        DIM = H * HD
        key = jax.random.key(seed)
        ks = jax.random.split(key, 5)
        s_in = 1.0 / np.sqrt(D_IN)
        s_d = 1.0 / np.sqrt(DIM)
        return {'data': jax.random.normal(ks[0], (N, L, D_IN), jnp.float32), 'W_qkv': jax.random.uniform(ks[1], (D_IN, 3 * DIM), jnp.float32, -s_in, s_in), 'b_qkv': jax.random.uniform(ks[2], (3 * DIM,), jnp.float32, -s_in, s_in), 'W_out': jax.random.uniform(ks[3], (DIM, D_OUT), jnp.float32, -s_d, s_d), 'b_out': jax.random.uniform(ks[4], (D_OUT,), jnp.float32, -s_d, s_d)}
    _L1_attn_in = _L1_attn_setup()

    def _L1_ffn_setup():
        import jax, jax.numpy as jnp
        import numpy as np
        E = 8
        K = 2
        CF = 1.25
        key = jax.random.key(seed)
        kx, kr, kg, ku, kd = jax.random.split(key, 5)
        D, F = (128, 512)
        x = jax.random.normal(kx, (4, 256, D), dtype=jnp.float32)
        router_w = 0.02 * jax.random.normal(kr, (E, D), dtype=jnp.float32)
        wg = jax.random.normal(kg, (E, D, F), dtype=jnp.float32) / np.sqrt(D)
        wu = jax.random.normal(ku, (E, D, F), dtype=jnp.float32) / np.sqrt(D)
        wd = jax.random.normal(kd, (E, F, D), dtype=jnp.float32) / np.sqrt(F)
        return {'x': x, 'router_w': router_w, 'wg': wg, 'wu': wu, 'wd': wd}
    _L1_ffn_in = _L1_ffn_setup()
    _d = {'L0_attn_x': _L0_attn_in['x'], 'L0_attn_w_qkv': _L0_attn_in['w_qkv'], 'L0_attn_w_out': _L0_attn_in['w_out'], 'L0_attn_b_out': _L0_attn_in['b_out'], 'L0_attn_ln_gamma': _L0_attn_in['ln_gamma'], 'L0_attn_ln_beta': _L0_attn_in['ln_beta'], 'L0_ffn_gate_w': _L0_ffn_in['gate_w'], 'L0_ffn_w_up': _L0_ffn_in['w_up'], 'L0_ffn_w_down': _L0_ffn_in['w_down'], 'L0_ffn_expert_bias': _L0_ffn_in['expert_bias'], 'L1_attn_W_qkv': _L1_attn_in['W_qkv'], 'L1_attn_b_qkv': _L1_attn_in['b_qkv'], 'L1_attn_W_out': _L1_attn_in['W_out'], 'L1_attn_b_out': _L1_attn_in['b_out'], 'L1_ffn_router_w': _L1_ffn_in['router_w'], 'L1_ffn_wg': _L1_ffn_in['wg'], 'L1_ffn_wu': _L1_ffn_in['wu'], 'L1_ffn_wd': _L1_ffn_in['wd']}
    _x0 = _d['L0_attn_x']
    _d['L0_attn_x'] = jax.random.normal(jax.random.fold_in(jax.random.key(seed), 1), (8, 512, 128), dtype=_x0.dtype)
    del _x0
    return _d

def reference(L0_attn_x, L0_attn_w_qkv, L0_attn_w_out, L0_attn_b_out, L0_attn_ln_gamma, L0_attn_ln_beta, L0_ffn_gate_w, L0_ffn_w_up, L0_ffn_w_down, L0_ffn_expert_bias, L1_attn_W_qkv, L1_attn_b_qkv, L1_attn_W_out, L1_attn_b_out, L1_ffn_router_w, L1_ffn_wg, L1_ffn_wu, L1_ffn_wd):

    def _L0_attn_ref(x, w_qkv, w_out, b_out, ln_gamma, ln_beta):
        import jax, jax.numpy as jnp
        import numpy as np
        HEADS = 32
        DIM_HEAD = 32
        EPS = 1e-06
        b, n, dim = x.shape
        scale = DIM_HEAD ** (-0.5)
        qkv = x @ w_qkv
        qkv = qkv.reshape(b, n, 3, HEADS, DIM_HEAD)
        qkv = jnp.transpose(qkv, (2, 0, 3, 1, 4))
        q, k, v = (qkv[0], qkv[1], qkv[2])
        dots = jnp.einsum('bhnd,bhmd->bhnm', q, k) * scale
        attn = jax.nn.softmax(dots, axis=-1)
        out = jnp.einsum('bhnm,bhmd->bhnd', attn, v)
        out = jnp.transpose(out, (0, 2, 1, 3)).reshape(b, n, HEADS * DIM_HEAD)
        out = out @ w_out + b_out
        mu = jnp.mean(out, axis=-1, keepdims=True)
        var = jnp.mean((out - mu) ** 2, axis=-1, keepdims=True)
        out = (out - mu) / jnp.sqrt(var + EPS) * ln_gamma + ln_beta
        return out

    def _L0_ffn_ref(x, gate_w, w_up, w_down, expert_bias):
        import jax, jax.numpy as jnp
        import numpy as np
        DIM = 128
        NUM_EXPERTS = 8
        TOP_K = 2
        HIDDEN = 4 * DIM // TOP_K
        BS, SLEN = (1, 256)

        def _moe(x, gate_w, w_up, w_down, expert_bias):
            bs, slen, dim = x.shape
            xf = x.reshape(-1, dim)
            scores = jax.nn.sigmoid(xf @ gate_w.T)
            biased = scores + expert_bias
            _, sel = jax.lax.top_k(biased, TOP_K)
            top_scores = jnp.take_along_axis(scores, sel, axis=-1)

            def body(acc, ew):
                e, wu, wd = ew
                w_t = jnp.sum(jnp.where(sel == e, top_scores, 0.0), axis=-1)
                xe = xf * w_t[:, None]
                h = jnp.square(jax.nn.relu(xe @ wu.T))
                return (acc + h @ wd.T, None)
            out0 = jnp.zeros_like(xf)
            out, _ = jax.lax.scan(body, out0, (jnp.arange(NUM_EXPERTS), w_up, w_down))
            return out.reshape(bs, slen, dim)
        return _moe(x, gate_w, w_up, w_down, expert_bias)

    def _L1_attn_ref(data, W_qkv, b_qkv, W_out, b_out):
        import jax, jax.numpy as jnp
        import numpy as np
        N, L, D_IN, H, HD, D_OUT = (4, 256, 128, 16, 64, 128)
        DIM = H * HD
        n, l = (data.shape[0], data.shape[1])
        qkv = data @ W_qkv + b_qkv
        q = qkv[:, :, :DIM].reshape(n, l, H, HD)
        k = qkv[:, :, DIM:2 * DIM].reshape(n, l, H, HD)
        v = qkv[:, :, 2 * DIM:].reshape(n, l, H, HD)
        scores = jnp.einsum('nqhd,nkhd->nhqk', q, k)
        attention = jax.nn.softmax(scores / jnp.sqrt(jnp.float32(HD)), axis=3)
        out = jnp.einsum('nhql,nlhd->nqhd', attention, v).reshape(n, l, DIM)
        return out @ W_out + b_out

    def _L1_ffn_ref(x, router_w, wg, wu, wd):
        import jax, jax.numpy as jnp
        import numpy as np
        E = 8
        K = 2
        CF = 1.25
        B, L, D = x.shape
        xf = x.reshape(-1, D)
        N = xf.shape[0]
        capacity = max(1, int(CF * N / E))
        logits = xf @ router_w.T
        probs = jax.nn.softmax(logits, axis=-1)
        topw, topi = jax.lax.top_k(probs, K)
        topw = topw / (topw.sum(-1, keepdims=True) + 1e-06)
        fe = topi.reshape(-1)
        fw = topw.reshape(-1)
        ft = jnp.repeat(jnp.arange(N), K)
        order = jnp.lexsort((-fw, fe))
        se, sw, st = (fe[order], fw[order], ft[order])
        counts = jax.ops.segment_sum(jnp.ones_like(se), se, num_segments=E)
        starts = jnp.cumsum(counts) - counts
        rank = jnp.arange(N * K) - starts[se]
        keep = rank < capacity
        pos = jnp.where(keep, rank, capacity)
        disp = jnp.zeros((E, capacity + 1, D), x.dtype).at[se, pos].set(xf[st])
        disp = disp[:, :capacity]
        g = jnp.einsum('ecd,edf->ecf', disp, wg)
        u = jnp.einsum('ecd,edf->ecf', disp, wu)
        eo = jnp.einsum('ecf,efd->ecd', jax.nn.silu(g) * u, wd)
        gathered = eo[se, jnp.minimum(pos, capacity - 1)]
        contrib = gathered * (sw * keep.astype(x.dtype))[:, None]
        out = jnp.zeros_like(xf).at[st].add(contrib)
        return out.reshape(B, L, D)
    x = L0_attn_x
    x = x + 0.5 * _L0_ffn_ref(_layernorm(x, axis=-1), L0_ffn_gate_w, L0_ffn_w_up, L0_ffn_w_down, L0_ffn_expert_bias)
    x = x + _L0_attn_ref(_layernorm(x, axis=-1), L0_attn_w_qkv, L0_attn_w_out, L0_attn_b_out, L0_attn_ln_gamma, L0_attn_ln_beta)
    x = x + 0.5 * _L0_ffn_ref(_layernorm(x, axis=-1), L0_ffn_gate_w, L0_ffn_w_up, L0_ffn_w_down, L0_ffn_expert_bias)
    x = x + 0.5 * _L1_ffn_ref(_layernorm(x, axis=-1), L1_ffn_router_w, L1_ffn_wg, L1_ffn_wu, L1_ffn_wd)
    x = x + _L1_attn_ref(_layernorm(x, axis=-1), L1_attn_W_qkv, L1_attn_b_qkv, L1_attn_W_out, L1_attn_b_out)
    x = x + 0.5 * _L1_ffn_ref(_layernorm(x, axis=-1), L1_ffn_router_w, L1_ffn_wg, L1_ffn_wu, L1_ffn_wd)
    return x

_drawn_inputs = setup_inputs


def setup_inputs(seed=0):
    import zlib

    import numpy as np

    out = dict(_drawn_inputs(seed))
    spreads = {'L0_attn_b_out': (0.0, 0.1),
     'L0_attn_ln_gamma': (1.0, 0.2),
     'L0_attn_ln_beta': (0.0, 0.1),
     'L0_ffn_expert_bias': (0.0, 0.34)}
    factors = {'L0_ffn_gate_w': 5.256, 'L0_ffn_w_up': 3.707, 'L1_attn_b_out': 3.444}
    for name, (base, spread) in spreads.items():
        noise = np.random.default_rng([zlib.crc32(name.encode()), seed]).standard_normal(out[name].shape)
        drawn = base * np.exp(spread * noise) if base else spread * noise
        out[name] = jnp.asarray(drawn.astype(out[name].dtype))
    for name, factor in factors.items():
        out[name] = (out[name] * factor).astype(out[name].dtype)
    return out
```

```python
import numpy as np
import concourse.bass as bass
from concourse import mybir
from contextlib import ExitStack

P = 128
DIM = 128
BATCHES = 8
SEQ = 512
TILES_B = SEQ // P
TILES = BATCHES * TILES_B
INNER = 1024
GROUPS = INNER // P
EXPERTS = 8
TOP_K = 2
HID0 = 256
HID1 = 512
CAP = int(1.25 * BATCHES * SEQ / EXPERTS)
SLOTS = EXPERTS * CAP
SLOT_TILES = CAP // P
HALF_CAP = CAP // 2
LN_EPS = 1e-5
OUT_EPS = 1e-6
TOPW_EPS = 1e-6
TOP_BIT = 29
OUTSIDE = 2 * SLOTS

C_IDENT = 0
C_BEFORE = C_IDENT + P
C_LOWER = C_BEFORE + P
C_SLOT0 = C_LOWER + EXPERTS * EXPERTS
C_WIDTH = C_SLOT0 + EXPERTS


def constants():
    c = np.zeros((P, C_WIDTH), np.float32)
    c[:, C_IDENT:C_BEFORE] = np.eye(P)
    c[:, C_BEFORE:C_LOWER] = np.triu(np.ones((P, P)), 1)
    c[:, C_LOWER:C_SLOT0] = np.tril(np.ones((EXPERTS, EXPERTS)), -1).reshape(-1)
    c[:, C_SLOT0:] = np.arange(EXPERTS) * CAP
    return c


def merge(*streams):
    live = [[s, n, 0.0] for s, n in streams]
    while live:
        live.sort(key=lambda x: x[2])
        first = live[0]
        if next(first[0], "end") == "end":
            live.remove(first)
        else:
            first[2] += 1.0 / first[1]


def build(nc, x, w_qkv0, w_out0, b_out0, gamma0, beta0, gate0, up0, down0, bias0,
          w_qkv1, b_qk1, b_v1, w_out1, b_out1, router1, wg1, wu1, wd1, consts, out,
          batches=BATCHES, stages=6):
    fp32 = mybir.dt.float32
    f32r = mybir.dt.float32r
    i32 = mybir.dt.int32
    u32 = mybir.dt.uint32
    ALU = mybir.AluOpType
    ACT = mybir.ActivationFunctionType
    AX = mybir.AxisListType

    ctx = ExitStack()
    with ctx:
        def sb(name, shape, dt=fp32):
            return ctx.enter_context(nc.sbuf_tensor(name, shape, dt))

        def sem(name):
            return ctx.enter_context(nc.semaphore(name))

        class Queue:

            def __init__(self, name):
                self.done = sem(f"{name}_done")
                self.count = 0
                self.steps = []

            def __call__(self, emit, *tickets, signal=True):
                if signal:
                    self.count += 1
                self.steps.append((emit, tickets, self.done if signal else None, 1))
                return (self.done, self.count) if signal else None

            def transfer(self, emit, arrival, *tickets):
                arrival.count += 16
                self.steps.append((emit, tickets, arrival.sem, 16))
                return (arrival.sem, arrival.count)

            def run(self, eng):
                waited = {}
                for emit, tickets, counter, by in self.steps:
                    for t in tickets:
                        if t is None:
                            continue
                        s, value = t
                        if waited.get(s.name, 0) < value:
                            eng.wait_ge(s, value)
                            waited[s.name] = value
                    ins = emit()
                    if counter is not None:
                        ins.then_inc(counter, by)

        class Arrival:

            def __init__(self, name):
                self.sem = sem(name)
                self.count = 0

            @property
            def all(self):
                return (self.sem, self.count)

        class Place:

            def __init__(self, ap):
                self.ap = ap
                self.free = ()

        class Ring:
            def __init__(self, aps):
                self.places = [Place(a) for a in aps]
                self.at = -1

            def take(self):
                self.at += 1
                return self.places[self.at % len(self.places)]

        pe, act, dve, pool, sp = (Queue(n) for n in ("pe", "act", "dve", "pool", "sp"))
        T_, S_, V_, G_, Y_ = nc.tensor, nc.scalar, nc.vector, nc.gpsimd, nc.sync

        X = sb("X", [P, TILES, DIM])
        cst = sb("cst", [P, C_WIDTH])
        ident = cst[:, C_IDENT:C_BEFORE]
        before = cst[:, C_BEFORE:C_LOWER]
        lower = cst[:, C_LOWER:C_SLOT0].rearrange("p (a e j) -> p a e j", a=1, e=EXPERTS)
        slot0 = cst[:, C_SLOT0:C_WIDTH].rearrange("p (a e) -> p a e", a=1)
        ones = sb("ones", [P, P])
        minus_half = sb("minus_half", [P, TILES_B])

        wqkv = sb("wqkv", [P, 3 * INNER])
        wout = sb("wout", [P, GROUPS, DIM])
        bqk = sb("bqk", [P, 2 * GROUPS])
        bv = sb("bv", [P, GROUPS])
        rows = sb("rows", [P, 4, DIM])
        gate_w = sb("gate_w", [P, EXPERTS])
        gate_b = sb("gate_b", [P, EXPERTS])
        router_w = sb("router_w", [P, EXPERTS])

        xn = [sb(f"xn{i}", [P, TILES_B, DIM]) for i in range(2)]
        xT = Ring([sb(f"xT{i}", [P, SEQ])[:, :] for i in range(2)])
        stats = [sb(f"stats{i}", [P, TILES_B, 6]) for i in range(2)]
        mv = [sb(f"mv{i}", [P, TILES_B, 2]) for i in range(2)]
        rstd = [sb(f"rstd{i}", [P, TILES_B]) for i in range(2)]

        ARENA = 25 * 1024
        arena = sb("arena", [P, ARENA])

        class Carve:
            def __init__(self):
                self.at = 0

            def __call__(self, *shape):
                n = int(np.prod(shape))
                ap = arena[:, self.at:self.at + n]
                self.at += n
                assert self.at <= ARENA, self.at
                if len(shape) == 1:
                    return ap
                names = " ".join("abcd"[:len(shape)])
                return ap.rearrange(f"p ({names}) -> p {names}", **dict(zip("abcd", shape)))

        psum = ctx.enter_context(nc.psum_tensor("psum", [P, 8, 512], fp32))
        bank = [psum[:, i, :] for i in range(8)]
        banks_a = Ring(bank[0:2])
        banks_b = Ring(bank[2:5])
        bank_pv = Ring(bank[5:6])
        banks_m = Ring(bank[6:8])

        slots_in = nc.dram_tensor("slots_in", (SLOTS, DIM), fp32, kind="Internal").ap()
        slots_out = nc.dram_tensor("slots_out", (SLOTS, DIM), fp32, kind="Internal").ap()

        got_x = [Arrival(f"got_x{b}") for b in range(2)]
        got_w = Arrival("got_w")
        got_w2 = Arrival("got_w2")
        got_small = Arrival("got_small")
        x_v = x.rearrange("b (t p) d -> b p t d", p=P)
        out_v = out.rearrange("b (t p) d -> b p t d", p=P)

        def load(dst, src, arrival, *tickets):
            return sp.transfer(lambda: Y_.dma_start(dst, src), arrival, *tickets)

        in_consts = load(cst[:, :], consts, Arrival("got_consts"))
        load(X[:, 0:TILES_B, :], x_v[0], got_x[0])
        first_batch = got_x[0].all
        for r, v in enumerate((b_out0, gamma0, beta0, b_out1)):
            load(rows[:, r, :], v.partition_broadcast(P), got_small)
        load(gate_b[:, :], bias0.partition_broadcast(P), got_small)
        load(gate_w[:, :], gate0, got_small)
        load(router_w[:, :], router1, got_small)
        load(bqk[:, :], b_qk1, got_small)
        load(bv[:, :], b_v1, got_small)
        small = got_small.all

        t_ones = dve(lambda: V_.memset(ones[:, :], 1.0))
        t_mh = dve(lambda: V_.memset(minus_half[:, :], -0.5))

        x_ready = [None] * batches

        class Norm:

            def __init__(self):
                self.n = 0
                self.xn_free = [(), ()]
                self.last = [None, None]

        norm_state = Norm()

        def moments(src_tiles, which, eps, *tickets):
            st, m, r = stats[which], mv[which], rstd[which]
            prev = norm_state.last[which]
            ts = []
            for t in range(TILES_B):
                ts.append(dve(lambda t=t: V_.bn_stats(st[:, t, :], src_tiles[t]), *tickets, prev))
            for t in range(TILES_B):
                last = dve(lambda t=t: V_.bn_aggr(m[:, t, :], st[:, t, :]), ts[t], prev)
            var = dve(lambda: V_.tensor_scalar(r[:, :], m[:, :, 1], eps, None, ALU.add), last, prev)
            root = pool(lambda: G_.tensor_tensor(r[:, :], r[:, :], minus_half[:, :], ALU.pow),
                        var, t_mh)
            return root

        def normalise(b, keep_rows=None):
            w = norm_state.n % 2
            norm_state.n += 1
            src = [X[:, b * TILES_B + t, :] for t in range(TILES_B)]
            root = moments(src, w, LN_EPS, x_ready[b])
            yield
            dst = xn[w][:, :, :] if keep_rows is None else keep_rows
            for t in range(TILES_B):
                normed = dve(lambda t=t: V_.tensor_scalar(dst[:, t, :], src[t], mv[w][:, t, 0:1],
                                                          rstd[w][:, t:t + 1], ALU.subtract, ALU.mult),
                             root, *norm_state.xn_free[w])
            norm_state.last[w] = normed
            yield
            bk = banks_m.take()
            for t in range(TILES_B):
                turned = pe(lambda t=t: T_.matmul(bk.ap[:, t * P:(t + 1) * P], dst[:, t, :], ident,
                                                  is_transpose=True),
                            normed, in_consts, *bk.free, signal=t == TILES_B - 1)
            norm_state.xn_free[w] = (turned,)
            place = xT.take()
            place.ready = act(lambda: S_.activation(place.ap, bk.ap, ACT.Copy), turned, *place.free)
            place.free = ()
            place.normed = normed
            bk.free = (place.ready,)
            normalise.place = place
            yield

        def drain(gen):
            for _ in gen:
                pass

        beats = sb("beats", [P, TILES_B, EXPERTS, EXPERTS])
        equal = sb("equal", [P, TILES_B, EXPERTS, EXPERTS])

        gate_last = [None]

        def ranks(value, rank, *tickets):
            vj = value.unsqueeze(2).to_broadcast([P, TILES_B, EXPERTS, EXPERTS])
            ve = value.unsqueeze(3).to_broadcast([P, TILES_B, EXPERTS, EXPERTS])
            low = lower.to_broadcast([P, TILES_B, EXPERTS, EXPERTS])
            a = dve(lambda: V_.tensor_tensor(beats[:, :, :, :], vj, ve, ALU.is_gt),
                    gate_last[0], *tickets)
            c = dve(lambda: V_.tensor_tensor(equal[:, :, :, :], vj, ve, ALU.is_equal), gate_last[0])
            c = dve(lambda: V_.tensor_tensor(equal[:, :, :, :], equal[:, :, :, :], low, ALU.mult),
                    c, in_consts)
            c = dve(lambda: V_.tensor_tensor(beats[:, :, :, :], beats[:, :, :, :],
                                             equal[:, :, :, :], ALU.add), a, c)
            c = dve(lambda: V_.tensor_reduce(rank, beats[:, :, :, :], AX.X, ALU.add), c)
            gate_last[0] = c
            return c

        gates = {n: [sb(f"{n}{i}", [P, TILES_B, EXPERTS]) for i in range(2)]
                 for n in ("score", "value", "rank", "weight")}
        gate_free = [(), ()]

        def logits(place, weights):
            bk = banks_m.take()
            for t in range(TILES_B):
                done = pe(lambda t=t: T_.matmul(bk.ap[:, t * EXPERTS:(t + 1) * EXPERTS],
                                                place.ap[:, t * P:(t + 1) * P], weights,
                                                start=True, stop=True),
                          place.ready, small, *bk.free, signal=t == TILES_B - 1)
            view = bk.ap[:, 0:TILES_B * EXPERTS].rearrange("p (t e) -> p t e", t=TILES_B)
            return bk, view, done

        def experts0(carve_free):
            carve = Carve()
            up = carve(EXPERTS * HID0)
            down = carve(EXPERTS, 2, DIM)
            hid = Ring([carve(2, SEQ) for _ in range(3)])
            w_up = load(up, up0, got_w, *carve_free)
            w_down = load(down, down0.rearrange("p (e c) d -> p e c d", e=EXPERTS), got_w2, *carve_free)
            gate = {}

            def prepare(b):
                yield from normalise(b)
                place = normalise.place
                g = b % 2
                score, value, rank, weight = (gates[n][g] for n in ("score", "value", "rank", "weight"))
                bk, view, done = logits(place, gate_w[:, :])
                yield
                s = act(lambda: S_.activation(score[:, :, :], view, ACT.Sigmoid), done, *gate_free[g])
                bk.free = (s,)
                bias = gate_b[:, :].unsqueeze(1).to_broadcast([P, TILES_B, EXPERTS])
                v = dve(lambda: V_.tensor_tensor(value[:, :, :], score[:, :, :], bias, ALU.add),
                        s, small, *gate_free[g])
                yield
                r = ranks(value[:, :, :], rank[:, :, :], v)
                yield
                v = dve(lambda: V_.scalar_tensor_tensor(out=value[:, :, :], in0=rank[:, :, :],
                                                        scalar=float(TOP_K), in1=score[:, :, :],
                                                        op0=ALU.is_lt, op1=ALU.mult), r)
                w = dve(lambda: V_.scalar_tensor_tensor(out=weight[:, :, :], in0=value[:, :, :],
                                                        scalar=0.5, in1=value[:, :, :],
                                                        op0=ALU.mult, op1=ALU.mult), v)
                gate[b] = (place, weight, w)
                yield

            def compute(b):
                place, weight, w = gate[b]
                steps = []

                def up_step(e):
                    h = hid.take()
                    squares = []
                    for c in range(2):
                        bk = banks_a.take()
                        col = (e * 2 + c) * P
                        u = pe(lambda bk=bk, col=col: T_.matmul(bk.ap, up[:, col:col + P], place.ap,
                                                                start=True, stop=True),
                               w_up, place.ready, *bk.free)
                        r = dve(lambda bk=bk, h=h, c=c: V_.tensor_scalar(h.ap[:, c, :], bk.ap, 0.0, None,
                                                                         ALU.max), u, *h.free)
                        bk.free = (r,)
                        squares.append(act(lambda h=h, c=c: S_.activation(h.ap[:, c, :], h.ap[:, c, :],
                                                                          ACT.Square), r))
                    if e == EXPERTS - 1:
                        place.free = (u,)
                    steps.append((h, squares))

                def down_step(e):
                    h, squares = steps[e]
                    bk = banks_b.take()
                    for t in range(TILES_B):
                        for c in range(2):
                            d = pe(lambda t=t, c=c: T_.matmul(bk.ap[:, t * P:(t + 1) * P],
                                                              h.ap[:, c, t * P:(t + 1) * P],
                                                              down[:, e, c, :],
                                                              start=c == 0, stop=c == 1),
                                   *squares, w_down, *bk.free, signal=t == TILES_B - 1 and c == 1)
                    h.free = (d,)
                    for t in range(TILES_B):
                        tile = b * TILES_B + t
                        a = dve(lambda t=t, tile=tile: V_.scalar_tensor_tensor(
                            out=X[:, tile, :], in0=bk.ap[:, t * P:(t + 1) * P],
                            scalar=weight[:, t, e:e + 1], in1=X[:, tile, :],
                            op0=ALU.mult, op1=ALU.add), d, w, x_ready[b])
                    bk.free = (a,)
                    x_ready[b] = a
                    return a

                up_step(0)
                yield
                for e in range(EXPERTS):
                    if e + 1 < EXPERTS:
                        up_step(e + 1)
                        yield
                    last = down_step(e)
                    yield
                gate_free[b % 2] = (last,)

            if x_ready[0] is None:
                x_ready[0] = first_batch
                for b in range(1, batches):
                    x_ready[b] = load(X[:, b * TILES_B:(b + 1) * TILES_B, :], x_v[b], Arrival(f"got_xb{b}"))
            drain(prepare(0))
            for b in range(batches):
                more = [(prepare(b + 1), 6)] if b + 1 < batches else []
                merge((compute(b), 16), *more)
            return (x_ready[batches - 1], (pe.done, pe.count), (dve.done, dve.count), (act.done, act.count))

        halves = {n: [sb(f"{n}{i}", [P, SEQ], f32r) for i in range(2)] for n in ("qh", "ql", "kh", "kl")}
        halves_free = [[], []]
        QS = [sb(f"QS{i}", [P, 4, SEQ], f32r) for i in range(2)]
        KS = [sb(f"KS{i}", [P, 4, SEQ], f32r) for i in range(2)]
        stack_free = [(), ()]
        stacked = [Arrival(f"stacked{i}") for i in range(2)]
        max_rows = [Arrival(f"max_rows{i}") for i in range(2)]
        V_grp = [sb(f"V{i}", [P, TILES_B, P]) for i in range(3)]
        v_free = [(), (), ()]
        top = [sb(f"top{i}", [P, 16]) for i in range(2)]
        top_free = [(), ()]
        mh = [sb(f"mh{i}", [16, P], f32r) for i in range(2)]
        ml = [sb(f"ml{i}", [16, P], f32r) for i in range(2)]
        m_free = [(), ()]
        stack_ones = [None]

        def attention(wqkv_src, wout_src, heads, width, bias_qk, finish, region_free):
            scale = float(width) ** -0.5
            stacks = 1 if width == 32 else 2
            carve = Carve()
            prob = Ring([carve(TILES_B, SEQ) for _ in range(2 * heads if heads == 4 else 4)])
            psum2 = Ring([carve(2, SEQ) for _ in range(4)])
            den = Ring([carve(SEQ) for _ in range(2)])
            OT = [carve(GROUPS, SEQ) for _ in range(1)]
            ot_free = [()]
            t_qkv = load(wqkv[:, :], wqkv_src, got_w, *region_free)
            t_wout = load(wout[:, :, :], wout_src, got_w, *region_free)
            t_w = got_w.all

            if stacks == 1:
                ones_at = [(i, slice(96, 98), slice(0, 4)) for i in range(2)]
            else:
                ones_at = [(i, slice(64, 66), slice(2, 4)) for i in range(2)]
            for i, rows_, at in ones_at:
                t_so = dve(lambda i=i, rows_=rows_, at=at: V_.memset(KS[i][rows_, at, :].bitcast(fp32), 1.0),
                           *stack_free[i])
            places = {}
            info = {}

            def front(b, g, n):
                i = n % 2
                place = places[b]
                qk_hl = []
                hf = tuple(halves_free[i])
                for which, (hi, lo) in enumerate((("qh", "ql"), ("kh", "kl"))):
                    bk = banks_m.take()
                    col = which * INNER + g * P
                    p_ = pe(lambda bk=bk, col=col: T_.matmul(bk.ap, wqkv[:, col:col + P], place.ap,
                                                             start=True, stop=True),
                            t_w, place.ready, *bk.free)
                    H, L = halves[hi][i], halves[lo][i]
                    if bias_qk:
                        bias = bqk[:, which * GROUPS + g:which * GROUPS + g + 1]
                        h_ = act(lambda bk=bk, H=H, bias=bias: S_.activation(H[:, :], bk.ap, ACT.Identity,
                                                                             bias=bias), p_, small, *hf)
                        l_ = dve(lambda bk=bk, H=H, L=L, bias=bias: V_.scalar_tensor_tensor(
                            out=L[:, :], in0=bk.ap, scalar=bias, in1=H[:, :].bitcast(fp32),
                            op0=ALU.add, op1=ALU.subtract), h_, *hf)
                    else:
                        h_ = act(lambda bk=bk, H=H: S_.activation(H[:, :], bk.ap, ACT.Copy), p_, *hf)
                        l_ = dve(lambda bk=bk, H=H, L=L: V_.tensor_tensor(
                            L[:, :], bk.ap, H[:, :].bitcast(fp32), ALU.subtract), h_, *hf)
                    bk.free = (l_,)
                    qk_hl += [h_, l_]
                    S = (QS, KS)[which][i]
                    waits = (h_, l_, *stack_free[i])
                    for h in range(heads):
                        src = slice(width * h, width * (h + 1))
                        if stacks == 1:
                            order = ((H, L, H), (H, H, L))[which]
                            for r, part in enumerate(order):
                                sp.transfer(lambda S=S, r=r, h=h, part=part, src=src: Y_.dma_start(
                                    S[32 * r:32 * r + 32, h, :].bitcast(fp32), part[src, :].bitcast(fp32)), stacked[i], *waits)
                        else:
                            order = ((H, 0, h), (L, 64, h), (H, 0, 2 + h)) if which == 0 else \
                                    ((H, 0, h), (H, 64, h), (L, 0, 2 + h))
                            for part, r, at in order:
                                sp.transfer(lambda S=S, r=r, at=at, part=part, src=src: Y_.dma_start(
                                    S[r:r + 64, at, :].bitcast(fp32), part[src, :].bitcast(fp32)), stacked[i], *waits)
                    yield
                t_stack = stacked[i].all
                halves_free[i][:] = [t_stack]
                bk = banks_m.take()
                for t in range(TILES_B):
                    p_ = pe(lambda t=t, bk=bk: T_.matmul(bk.ap[:, t * P:(t + 1) * P],
                                                         place.ap[:, t * P:(t + 1) * P],
                                                         wqkv[:, 2 * INNER + g * P:2 * INNER + (g + 1) * P],
                                                         start=True, stop=True),
                            t_w, place.ready, *bk.free, signal=t == TILES_B - 1)
                if g == GROUPS - 1:
                    place.free = (p_,)
                v_ = act(lambda bk=bk: S_.activation(V_grp[n % 3][:, :, :], bk.ap.rearrange(
                    "p (t f) -> p t f", t=TILES_B), ACT.Copy), p_, *v_free[n % 3])
                bk.free = (v_,)
                yield
                for h in range(heads):
                    for qt in range(TILES_B):
                        bk = banks_a.take()
                        q = slice(qt * P, (qt + 1) * P)
                        if stacks == 1:
                            s_ = pe(lambda bk=bk, h=h, q=q: T_.matmul(bk.ap, QS[i][0:96, h, q],
                                                                      KS[i][0:96, h, :],
                                                                      start=True, stop=True),
                                    t_stack, *bk.free)
                        else:
                            pe(lambda bk=bk, h=h, q=q: T_.matmul(bk.ap, QS[i][:, h, q], KS[i][:, h, :],
                                                                 start=True, stop=False),
                               t_stack, *bk.free, signal=False)
                            s_ = pe(lambda bk=bk, h=h, q=q: T_.matmul(bk.ap, QS[i][0:64, 2 + h, q],
                                                                      KS[i][0:64, 2 + h, :],
                                                                      start=False, stop=True))
                        m_ = dve(lambda bk=bk, h=h, qt=qt: V_.reduce_max(
                            top[i][:, h * TILES_B + qt:h * TILES_B + qt + 1], bk.ap, AX.X),
                            s_, *top_free[i])
                        bk.free = (m_,)
                        yield
                n_top = heads * TILES_B
                bk = banks_m.take()
                t_ = pe(lambda bk=bk: T_.matmul(bk.ap[0:n_top, 0:P], top[i][:, 0:n_top], ident,
                                                is_transpose=True), m_, *bk.free)
                top_free[i] = (t_,)
                a_ = act(lambda bk=bk: S_.activation(mh[i][0:n_top, :], bk.ap[0:n_top, 0:P], ACT.Copy,
                                                     scale=-1.0), t_, *m_free[i])
                b_ = dve(lambda bk=bk: V_.scalar_tensor_tensor(
                    out=ml[i][0:n_top, :], in0=bk.ap[0:n_top, 0:P], scalar=-1.0,
                    in1=mh[i][0:n_top, :].bitcast(fp32), op0=ALU.mult, op1=ALU.subtract),
                    a_, *m_free[i])
                bk.free = (b_,)
                base, at0 = (96, 0) if stacks == 1 else (64, 2)
                for r, part in enumerate((mh[i], ml[i])):
                    for h in range(heads):
                        sp.transfer(lambda r=r, h=h, part=part: Y_.dma_start(
                            QS[i][base + r:base + r + 1, at0 + h, :].rearrange(
                                "a (t q) -> a t q", t=TILES_B).bitcast(fp32),
                            part[h * TILES_B:(h + 1) * TILES_B, :].bitcast(fp32)), max_rows[i], a_, b_)
                m_free[i] = (max_rows[i].all,)
                info[n] = dict(t_max=max_rows[i].all, t_stack=t_stack, v=v_)
                yield

            def middle(b, g, n):
                i = n % 2
                d = info[n]
                d["prob"], d["sum"] = [], []
                for h in range(heads):
                    pr = prob.take()
                    es = []
                    for kt in range(TILES_B):
                        bk = banks_b.take()
                        k = slice(kt * P, (kt + 1) * P)
                        if stacks == 1:
                            s_ = pe(lambda bk=bk, h=h, k=k: T_.matmul(bk.ap, KS[i][0:98, h, k],
                                                                      QS[i][0:98, h, :],
                                                                      start=True, stop=True),
                                    d["t_max"], d["t_stack"], t_so, *bk.free)
                        else:
                            pe(lambda bk=bk, h=h, k=k: T_.matmul(bk.ap, KS[i][:, h, k], QS[i][:, h, :],
                                                                 start=True, stop=False),
                               d["t_stack"], *bk.free, signal=False)
                            s_ = pe(lambda bk=bk, h=h, k=k: T_.matmul(bk.ap, KS[i][0:66, 2 + h, k],
                                                                      QS[i][0:66, 2 + h, :],
                                                                      start=False, stop=True),
                                    d["t_max"], t_so)
                        e_ = act(lambda bk=bk, pr=pr, kt=kt: S_.activation(pr.ap[:, kt, :], bk.ap,
                                                                           ACT.Exp, scale=scale),
                                 s_, *pr.free)
                        bk.free = (e_,)
                        es.append(e_)
                        yield
                    s2 = psum2.take()
                    a_ = pool(lambda pr=pr, s2=s2: G_.tensor_tensor(s2.ap, pr.ap[:, 0:2, :],
                                                                    pr.ap[:, 2:4, :], ALU.add),
                              e_, *s2.free)
                    d["prob"].append((pr, e_, a_))
                    d["sum"].append((s2, a_))
                stack_free[i] = (s_,)

            def back(b, g, n):
                i = n % 2
                d = info.pop(n)
                dn = banks_m.take()
                for half in range(2):
                    for h in range(heads):
                        s2, a_ = d["sum"][h]
                        c = slice(width * h, width * (h + 1))
                        n_ = pe(lambda half=half, c=c, s2=s2, h=h: T_.matmul(
                            dn.ap[c, :], ones[:, 0:width], s2.ap[:, half, :],
                            start=half == 0, stop=half == 1, tile_position=(0, width * h)),
                            a_, t_ones, *dn.free)
                        if half == 1:
                            s2.free = (n_,)
                r = den.take()
                r_ = dve(lambda: V_.reciprocal(r.ap, dn.ap), n_, *r.free)
                dn.free = (r_,)
                yield
                o = bank_pv.take()
                for kt in range(TILES_B):
                    for h in range(heads):
                        c = slice(width * h, width * (h + 1))
                        pr, e_, a_ = d["prob"][h]
                        v_ = pe(lambda kt=kt, c=c, pr=pr, h=h: T_.matmul(
                            o.ap[c, :], V_grp[n % 3][:, kt, c], pr.ap[:, kt, :],
                            start=kt == 0, stop=kt == TILES_B - 1, tile_position=(0, width * h)),
                            e_, d["v"], *o.free, signal=kt == TILES_B - 1)
                        if kt == TILES_B - 1:
                            pr.free = (v_, a_)
                    yield
                v_free[n % 3] = (v_,)
                o_ = dve(lambda: V_.tensor_tensor(OT[0][:, g, :], o.ap, r.ap, ALU.mult),
                         v_, r_, *ot_free[0])
                o.free = (o_,)
                r.free = (o_,)
                if bias_qk:
                    o_ = dve(lambda: V_.tensor_scalar(OT[0][:, g, :], OT[0][:, g, :], bv[:, g:g + 1],
                                                      None, ALU.add), o_, small)
                yield
                if g == GROUPS - 1:
                    bk = banks_m.take()
                    for t in range(TILES_B):
                        for gg in range(GROUPS):
                            p_ = pe(lambda t=t, gg=gg: T_.matmul(bk.ap[:, t * P:(t + 1) * P],
                                                                 OT[0][:, gg, t * P:(t + 1) * P],
                                                                 wout[:, gg, :],
                                                                 start=gg == 0, stop=gg == GROUPS - 1),
                                    o_, t_w, *bk.free,
                                    signal=t == TILES_B - 1 and gg == GROUPS - 1)
                    ot_free[0] = (p_,)
                    finish(b, bk, p_)
                    yield

            order = [(b, g) for b in range(batches) for g in range(GROUPS)]
            drain(normalise(0))
            places[0] = normalise.place
            n_front = 3 + heads * TILES_B + 1
            for n in range(len(order) + 2):
                streams = []
                if n - 2 >= 0:
                    streams.append((back(*order[n - 2], n - 2), TILES_B + 3))
                if 0 <= n - 1 < len(order):
                    streams.append((middle(*order[n - 1], n - 1), heads * TILES_B))
                if n < len(order):
                    b, g = order[n]
                    streams.append((front(b, g, n), n_front))
                    if g == GROUPS - 2 and b + 1 < batches:
                        def ahead(b=b):
                            yield from normalise(b + 1)
                            places[b + 1] = normalise.place
                        streams.append((ahead(), 3))
                merge(*streams)
            return ((pe.done, pe.count), (dve.done, dve.count), (act.done, act.count),
                    (pool.done, pool.count), stacked[0].all, stacked[1].all, max_rows[0].all,
                    max_rows[1].all)

        y = [sb("y", [P, TILES_B, DIM])]
        y_free = [()]

        def row(r):
            return rows[:, r, :].unsqueeze(1).to_broadcast([P, TILES_B, DIM])

        def finish0(b, bk, p_):
            i = 0
            view = bk.ap.rearrange("p (t d) -> p t d", t=TILES_B)
            a = dve(lambda: V_.tensor_tensor(y[i][:, :, :], view, row(0), ALU.add), p_, small, *y_free[i])
            bk.free = (a,)
            w = norm_state.n % 2
            norm_state.n += 1
            root = moments([y[i][:, t, :] for t in range(TILES_B)], w, OUT_EPS, a)
            for t in range(TILES_B):
                a = dve(lambda t=t: V_.tensor_scalar(y[i][:, t, :], y[i][:, t, :], mv[w][:, t, 0:1],
                                                     rstd[w][:, t:t + 1], ALU.subtract, ALU.mult), root)
            norm_state.last[w] = a
            a = dve(lambda: V_.tensor_tensor(y[i][:, :, :], y[i][:, :, :], row(1), ALU.mult), a)
            a = dve(lambda: V_.tensor_tensor(y[i][:, :, :], y[i][:, :, :], row(2), ALU.add), a)
            xb = X[:, b * TILES_B:(b + 1) * TILES_B, :]
            a = dve(lambda: V_.tensor_tensor(xb, xb, y[i][:, :, :], ALU.add), a, x_ready[b])
            y_free[i] = (a,)
            x_ready[b] = a

        def finish1(b, bk, p_):
            i = 0
            view = bk.ap.rearrange("p (t d) -> p t d", t=TILES_B)
            a = dve(lambda: V_.tensor_tensor(y[i][:, :, :], view, row(3), ALU.add), p_, small, *y_free[i])
            bk.free = (a,)
            xb = X[:, b * TILES_B:(b + 1) * TILES_B, :]
            a = dve(lambda: V_.tensor_tensor(xb, xb, y[i][:, :, :], ALU.add), a, x_ready[b])
            y_free[i] = (a,)
            x_ready[b] = a

        gathered = [Arrival(f"gathered{i}") for i in range(4)]
        scattered = Arrival("scattered")
        zeroed = Arrival("zeroed")
        slots_loaded = [Arrival(f"slots_loaded{i}") for i in range(2)]
        slots_stored = [Arrival(f"slots_stored{i}") for i in range(2)]
        dram_free = [()]
        tiles = batches * TILES_B

        def experts1(region_free):
            carve = Carve()
            wg = carve(EXPERTS // 2, HID1)
            wu = carve(EXPERTS // 2, HID1)
            wd = carve(EXPERTS // 2, HID1 // P, DIM)
            XN = carve(TILES, DIM)
            W = carve(tiles, EXPERTS)
            R = carve(tiles, EXPERTS)
            ge = carve(tiles, EXPERTS)
            flags = carve(2, tiles, EXPERTS)
            scan = [carve(2, tiles, EXPERTS) for _ in range(2)]
            tmp = [carve(tiles, EXPERTS) for _ in range(3)]
            cnt = carve(EXPERTS)
            thr, cand, step = (carve(EXPERTS) for _ in range(3))
            slot_k = carve(2, tiles)
            kept_k = carve(2, tiles)
            w_k = carve(2, tiles)
            idx_out = carve(2, tiles)
            idx_in = carve(2, tiles)
            dst_t = Ring([carve(CAP) for _ in range(2)])
            rows_in = [carve(SLOT_TILES, DIM) for _ in range(2)]
            rows_free = [(), ()]
            sig = Ring([carve(HALF_CAP) for _ in range(3)])
            hid = Ring([carve(HID1 // P, CAP) for _ in range(1)])
            eo = Ring([carve(SLOT_TILES, DIM) for _ in range(2)])
            got = [carve(DIM) for _ in range(8)]
            got_free = [()] * 8
            soft = [carve(TILES_B) for _ in range(4)]

            t_wt = {}
            wt_free = [()] * 4

            def load_weights(e):
                i = e % 4
                a = Arrival(f"we{len(we_sems)}") if len(we_sems) < 4 else we_sems[i]
                if len(we_sems) < 4:
                    we_sems.append(a)
                waits = (*region_free, *wt_free[i])
                load(wg[:, i, :], wg1[:, e, :], a, *waits)
                load(wu[:, i, :], wu1[:, e, :], a, *waits)
                load(wd[:, i, :, :], wd1[:, e, :, :], a, *waits)
                t_wt[e] = a.all

            for e in range(4):
                load_weights(e)

            soft_free = [None]

            def route(b):
                yield from normalise(b, XN[:, b * TILES_B:(b + 1) * TILES_B, :])
                place = normalise.place
                g = b % 2
                score, value = (gates[n][g] for n in ("score", "value"))
                bk, view, done = logits(place, router_w[:, :])
                place.free = (done,)
                yield
                here = slice(b * TILES_B, (b + 1) * TILES_B)
                wide = [P, TILES_B, EXPERTS]
                top_, sum_, sel_, inv_ = soft
                f = soft_free[0]
                a = dve(lambda: V_.tensor_reduce(top_, view, AX.X, ALU.max), done, f)
                a = dve(lambda: V_.tensor_tensor(value[:, :, :], view, top_.unsqueeze(2).to_broadcast(wide),
                                                 ALU.subtract), a, *gate_free[g])
                bk.free = (a,)
                e_ = act(lambda: S_.activation(score[:, :, :], value[:, :, :], ACT.Exp), a)
                a = dve(lambda: V_.tensor_reduce(sum_, score[:, :, :], AX.X, ALU.add), e_, f)
                a = dve(lambda: V_.reciprocal(inv_, sum_), a)
                a = dve(lambda: V_.tensor_tensor(score[:, :, :], score[:, :, :],
                                                 inv_.unsqueeze(2).to_broadcast(wide), ALU.mult), a)
                yield
                a = ranks(score[:, :, :], R[:, here, :], a, *region_free)
                a = dve(lambda: V_.scalar_tensor_tensor(out=value[:, :, :], in0=R[:, here, :],
                                                        scalar=float(TOP_K), in1=score[:, :, :],
                                                        op0=ALU.is_lt, op1=ALU.mult), a)
                a = dve(lambda: V_.tensor_reduce(sel_, value[:, :, :], AX.X, ALU.add), a)
                a = dve(lambda: V_.tensor_scalar(sel_, sel_, TOPW_EPS, None, ALU.add), a)
                a = dve(lambda: V_.reciprocal(inv_, sel_), a)
                a = dve(lambda: V_.tensor_tensor(W[:, here, :], value[:, :, :],
                                                 inv_.unsqueeze(2).to_broadcast(wide), ALU.mult), a)
                soft_free[0] = a
                gate_free[g] = (a,)
                yield
                route.last = a

            for b in range(batches):
                drain(route(b))
            a = route.last

            def bits(v):
                return v.bitcast(i32)

            wide = [P, tiles, EXPERTS]
            a = dve(lambda: V_.memset(bits(thr), 0), a)
            for bit in range(TOP_BIT, -1, -1):
                a = dve(lambda bit=bit: V_.tensor_scalar(bits(cand), bits(thr), 1 << bit, None,
                                                         ALU.bitwise_or), a)
                a = dve(lambda: V_.tensor_tensor(ge, W, cand.unsqueeze(1).to_broadcast(wide),
                                                 ALU.is_ge), a)
                a = dve(lambda: V_.tensor_reduce(cnt, ge.rearrange("p t e -> p e t"), AX.X, ALU.add), a)
                bk = banks_m.take()
                c_ = pe(lambda bk=bk: T_.matmul(bk.ap[:, 0:EXPERTS], ones[:, :], cnt,
                                                start=True, stop=True), a, t_ones, *bk.free)
                a = dve(lambda bk=bk, bit=bit: V_.tensor_scalar(bits(step), bk.ap[:, 0:EXPERTS],
                                                                float(CAP), float(1 << bit),
                                                                ALU.is_ge, ALU.mult), c_)
                bk.free = (a,)
                a = dve(lambda: V_.tensor_tensor(bits(thr), bits(thr), bits(step), ALU.bitwise_or), a)

            thr_b = thr.unsqueeze(1).to_broadcast(wide)
            over, tied = flags[:, 0], flags[:, 1]
            a0 = dve(lambda: V_.tensor_tensor(over, W, thr_b, ALU.is_gt), a)
            a = dve(lambda: V_.tensor_tensor(tied, W, thr_b, ALU.is_equal), a)
            a = dve(lambda: V_.scalar_tensor_tensor(out=tied, in0=W, scalar=0.0, in1=tied,
                                                    op0=ALU.is_gt, op1=ALU.mult), a)
            flat = "p a t e -> p (a t e)"
            inside, totals = banks_b.take(), banks_b.take()
            n_flags = 2 * tiles * EXPERTS
            i_ = pe(lambda: T_.matmul(inside.ap[:, 0:n_flags], before, flags.rearrange(flat),
                                      start=True, stop=True), a0, a, in_consts, *inside.free)
            t_ = pe(lambda: T_.matmul(totals.ap[:, 0:n_flags], ones[:, :], flags.rearrange(flat),
                                      start=True, stop=True), *totals.free)
            a = dve(lambda: V_.tensor_copy(scan[0].rearrange(flat), totals.ap[:, 0:n_flags]), t_)
            totals.free = (a,)
            s, shift = 0, 1
            while shift < tiles:
                src, dst = scan[s], scan[1 - s]
                b1 = dve(lambda src=src, dst=dst, k=shift: V_.tensor_tensor(
                    dst[:, :, k:, :], src[:, :, k:, :], src[:, :, :tiles - k, :], ALU.add), a)
                a = dve(lambda src=src, dst=dst, k=shift: V_.tensor_copy(
                    dst[:, :, :k, :], src[:, :, :k, :]), b1)
                s, shift = 1 - s, shift * 2
            upto, pos = scan[s], scan[1 - s]
            a = dve(lambda: V_.tensor_copy(pos.rearrange(flat), inside.ap[:, 0:n_flags]), a, i_)
            inside.free = (a,)
            if tiles > 1:
                a = dve(lambda: V_.tensor_tensor(pos[:, :, 1:, :], pos[:, :, 1:, :],
                                                 upto[:, :, :tiles - 1, :], ALU.add), a)
            all_over = upto[:, 0, tiles - 1:tiles, :].to_broadcast(wide)
            pos_o, pos_t = pos[:, 0], pos[:, 1]
            a = dve(lambda: V_.tensor_tensor(pos_t, pos_t, all_over, ALU.add), a)
            a = dve(lambda: V_.scalar_tensor_tensor(out=tied, in0=pos_t, scalar=float(CAP), in1=tied,
                                                    op0=ALU.is_lt, op1=ALU.mult), a)
            m0, m1, m2 = tmp
            kept = ge
            a = dve(lambda: V_.tensor_tensor(m0, over, pos_o, ALU.mult), a)
            a = dve(lambda: V_.tensor_tensor(m1, tied, pos_t, ALU.mult), a)
            a = dve(lambda: V_.tensor_tensor(m0, m0, m1, ALU.add), a)
            a = dve(lambda: V_.tensor_tensor(m0, m0, slot0.to_broadcast(wide), ALU.add), a)
            a = dve(lambda: V_.tensor_tensor(kept, over, tied, ALU.add), a)
            for k in range(TOP_K):
                a = dve(lambda k=k: V_.scalar_tensor_tensor(out=m1, in0=R, scalar=float(k), in1=kept,
                                                            op0=ALU.is_equal, op1=ALU.mult), a)
                a = dve(lambda k=k: V_.tensor_reduce(kept_k[:, k, :], m1, AX.X, ALU.add), a)
                a = dve(lambda k=k: V_.tensor_tensor(m2, m1, m0, ALU.mult), a)
                a = dve(lambda k=k: V_.tensor_reduce(slot_k[:, k, :], m2, AX.X, ALU.add), a)
                a = dve(lambda k=k: V_.tensor_tensor(m2, m1, W, ALU.mult), a)
                a = dve(lambda k=k: V_.tensor_reduce(w_k[:, k, :], m2, AX.X, ALU.add), a)
            a = dve(lambda: V_.tensor_scalar(w_k, w_k, 0.5, None, ALU.mult), a)
            a = dve(lambda: V_.tensor_copy(bits(idx_in), slot_k), a)
            a = dve(lambda: V_.tensor_scalar(kept_k, kept_k, -float(OUTSIDE), float(OUTSIDE),
                                             ALU.mult, ALU.add), a)
            a = dve(lambda: V_.tensor_tensor(bits(idx_out), slot_k, kept_k, ALU.add), a)
            t_idx = a

            for t in range(tiles):
                for k in range(TOP_K):
                    pool.transfer(lambda t=t, k=k: G_.indirect_dma_start(
                        slots_in, bass.IndirectOffsetOnAxis(ap=idx_out[:, k, t:t + 1].bitcast(u32), axis=0),
                        XN[:, t, :], None, bounds_check=SLOTS - 1, oob_is_err=False),
                        scattered, t_idx, zeroed.all, *dram_free[0])

            in_v = slots_in.rearrange("(e s p) d -> e p s d", e=EXPERTS, p=P)
            out_slots = slots_out.rearrange("(e s p) d -> e p s d", e=EXPERTS, p=P)

            def load_rows(e):
                i = e % 2
                return load(rows_in[i], in_v[e], slots_loaded[i], scattered.all, *rows_free[i])

            t_rows = {0: load_rows(0)}
            for e in range(EXPERTS):
                i, wi = e % 2, e % 4
                if e + 1 < EXPERTS:
                    t_rows[e + 1] = load_rows(e + 1)
                dT = dst_t.take()
                cps = []
                for part, (lo_, hi_) in enumerate(((0, 4), (4, SLOT_TILES))):
                    bk = banks_m.take()
                    for s_ in range(lo_, hi_):
                        c_ = pe(lambda bk=bk, s_=s_, lo_=lo_, i=i: T_.matmul(
                            bk.ap[:, (s_ - lo_) * P:(s_ - lo_ + 1) * P], rows_in[i][:, s_, :], ident,
                            is_transpose=True), t_rows[e], *bk.free, signal=s_ == hi_ - 1)
                    n = (hi_ - lo_) * P
                    cp = dve(lambda bk=bk, dT=dT, lo_=lo_, n=n: V_.tensor_copy(
                        dT.ap[:, lo_ * P:lo_ * P + n], bk.ap[:, 0:n]), c_, *dT.free)
                    bk.free = (cp,)
                    cps.append(cp)
                rows_free[i] = (c_,)
                h = hid.take()
                for f in range(HID1 // P):
                    for half in range(2):
                        cols = slice(half * HALF_CAP, (half + 1) * HALF_CAP)
                        gb, ub = banks_a.take(), banks_b.take()
                        g_ = pe(lambda gb=gb, f=f, cols=cols, dT=dT, wi=wi: T_.matmul(
                            gb.ap[:, 0:HALF_CAP], wg[:, wi, f * P:(f + 1) * P], dT.ap[:, cols],
                            start=True, stop=True), *cps, t_wt[e], *gb.free)
                        u_ = pe(lambda ub=ub, f=f, cols=cols, dT=dT, wi=wi: T_.matmul(
                            ub.ap[:, 0:HALF_CAP], wu[:, wi, f * P:(f + 1) * P], dT.ap[:, cols],
                            start=True, stop=True), *ub.free)
                        sg = sig.take()
                        s_ = act(lambda sg=sg, gb=gb: S_.activation(sg.ap, gb.ap[:, 0:HALF_CAP], ACT.Silu),
                                 g_, *sg.free)
                        gb.free = (s_,)
                        m_ = dve(lambda sg=sg, ub=ub, h=h, f=f, cols=cols: V_.tensor_tensor(
                            h.ap[:, f, cols], ub.ap[:, 0:HALF_CAP], sg.ap, ALU.mult), s_, u_, *h.free)
                        ub.free = (m_,)
                        sg.free = (m_,)
                dT.free = (u_,)
                o = eo.take()
                outs = []
                for part, (lo_, hi_) in enumerate(((0, 4), (4, SLOT_TILES))):
                    bk = banks_m.take()
                    for s_ in range(lo_, hi_):
                        for f in range(HID1 // P):
                            d_ = pe(lambda bk=bk, s_=s_, lo_=lo_, f=f, h=h, wi=wi: T_.matmul(
                                bk.ap[:, (s_ - lo_) * P:(s_ - lo_ + 1) * P],
                                h.ap[:, f, s_ * P:(s_ + 1) * P], wd[:, wi, f, :],
                                start=f == 0, stop=f == HID1 // P - 1), m_, *bk.free,
                                signal=s_ == hi_ - 1 and f == HID1 // P - 1)
                    n = (hi_ - lo_) * P
                    c_ = act(lambda bk=bk, o=o, lo_=lo_, hi_=hi_, n=n: S_.activation(
                        o.ap[:, lo_:hi_, :], bk.ap[:, 0:n].rearrange("p (s d) -> p s d", d=DIM), ACT.Copy),
                        d_, *o.free)
                    bk.free = (c_,)
                h.free = (d_,)
                wt_free[wi] = (d_,)
                o.free = (sp.transfer(lambda o=o, e=e: Y_.dma_start(out_slots[e], o.ap),
                                      slots_stored[i], c_),)
                if e + 4 < EXPERTS:
                    load_weights(e + 4)
            stored = (slots_stored[0].all, slots_stored[1].all)
            for t in range(tiles):
                b = t // TILES_B
                for k in range(TOP_K):
                    n = (t * TOP_K + k)
                    j = n % 8
                    r = gathered8[j]
                    g_ = pool.transfer(lambda t=t, k=k, j=j: G_.indirect_dma_start(
                        got[j], None, slots_out,
                        bass.IndirectOffsetOnAxis(ap=idx_in[:, k, t:t + 1].bitcast(u32), axis=0),
                        bounds_check=SLOTS - 1, oob_is_err=False), r, *stored, *got_free[j])
                    a = dve(lambda t=t, k=k, j=j: V_.scalar_tensor_tensor(
                        out=X[:, t, :], in0=got[j], scalar=w_k[:, k, t:t + 1], in1=X[:, t, :],
                        op0=ALU.mult, op1=ALU.add), g_, x_ready[b], a)
                    got_free[j] = (a,)
                x_ready[b] = a
            dram_free[0] = (a, t_rows[EXPERTS - 1], t_rows[EXPERTS - 2], *stored)
            return (a, (pe.done, pe.count), (act.done, act.count), scattered.all, *stored)

        we_sems = []
        gathered8 = [Arrival(f"gath{i}") for i in range(8)]

        zero_v = slots_in.rearrange("(n p) d -> p n d", p=P)
        zeros = sb("zeros", [P, DIM])
        t_z = dve(lambda: V_.memset(zeros[:, :], 0.0))
        act.transfer(lambda: S_.dma_start(zero_v, zeros[:, :].unsqueeze(1).to_broadcast(
            [P, SLOTS // P, DIM])), zeroed, t_z)

        free = ()
        if stages >= 1:
            free = experts0(free)
        if stages >= 2:
            free = attention(w_qkv0, w_out0, 4, 32, False, finish0, free)
        if stages >= 3:
            free = experts0(free)
        if stages >= 4:
            free = experts1(free)
        if stages >= 5:
            free = attention(w_qkv1, w_out1, 2, 64, True, finish1, free)
        if stages >= 6:
            free = experts1(free)
        stored = Arrival("stored")
        for b in range(batches):
            sp.transfer(lambda b=b: Y_.dma_start(out_v[b], X[:, b * TILES_B:(b + 1) * TILES_B, :]),
                        stored, x_ready[b])

        block = ctx.enter_context(nc.Block())

        @block.tensor
        def _(eng):
            pe.run(eng)

        @block.scalar
        def _(eng):
            act.run(eng)

        @block.vector
        def _(eng):
            dve.run(eng)

        @block.gpsimd
        def _(eng):
            pool.run(eng)

        @block.sync
        def _(eng):
            sp.run(eng)
            eng.wait_ge(stored.sem, stored.count)
            for a in (zeroed, scattered, *slots_stored):
                if a.count:
                    eng.wait_ge(a.sem, a.count)


def lay_out(inputs):
    f = {k: np.asarray(v) for k, v in inputs.items()}
    w1, b1 = f["L1_attn_W_qkv"], f["L1_attn_b_qkv"]
    a = {
        "x": f["L0_attn_x"],
        "w_qkv0": f["L0_attn_w_qkv"],
        "w_out0": f["L0_attn_w_out"].reshape(GROUPS, P, DIM).transpose(1, 0, 2),
        "b_out0": f["L0_attn_b_out"], "gamma0": f["L0_attn_ln_gamma"], "beta0": f["L0_attn_ln_beta"],
        "gate0": f["L0_ffn_gate_w"].T,
        "up0": f["L0_ffn_w_up"].transpose(2, 0, 1).reshape(DIM, EXPERTS * HID0),
        "down0": f["L0_ffn_w_down"].transpose(2, 0, 1).reshape(2, P, EXPERTS, DIM)
                  .transpose(1, 2, 0, 3).reshape(P, EXPERTS * 2, DIM),
        "bias0": f["L0_ffn_expert_bias"],
        "w_qkv1": w1,
        "b_qk1": b1[:2 * INNER].reshape(2 * GROUPS, P).T,
        "b_v1": b1[2 * INNER:].reshape(GROUPS, P).T,
        "w_out1": f["L1_attn_W_out"].reshape(GROUPS, P, DIM).transpose(1, 0, 2),
        "b_out1": f["L1_attn_b_out"],
        "router1": f["L1_ffn_router_w"].T,
        "wg1": f["L1_ffn_wg"].transpose(1, 0, 2),
        "wu1": f["L1_ffn_wu"].transpose(1, 0, 2),
        "wd1": f["L1_ffn_wd"].reshape(EXPERTS, HID1 // P, P, DIM).transpose(2, 0, 1, 3),
        "consts": constants(),
    }
    return {k: np.ascontiguousarray(v) for k, v in a.items()}


def kernel(**inputs):
    import concourse.bacc as _bacc
    from concourse.bass_utils import run_bass_kernel_spmd as _run

    nc = _bacc.Bacc("TRN2", target_bir_lowering=False, num_devices=1)
    arrays, args = {}, {}
    for name, a in lay_out(inputs).items():
        arrays[f"in_{name}"] = a
        args[name] = nc.dram_tensor(f"in_{name}", a.shape, mybir.dt.from_np(a.dtype),
                                    kind="ExternalInput").ap()
    out = nc.dram_tensor("out", (BATCHES, SEQ, DIM), mybir.dt.float32, kind="ExternalOutput").ap()
    build(nc, **args, out=out)
    return _run(nc, [arrays], core_ids=[0]).results[0]["out"]
```

```python
import numpy as np
import concourse.bass as bass
from concourse import mybir
from contextlib import ExitStack

P = 128
DIM = 128
BATCHES = 8
SEQ = 512
TILES_B = SEQ // P
TILES = BATCHES * TILES_B
INNER = 1024
GROUPS = INNER // P
EXPERTS = 8
TOP_K = 2
HID0 = 256
HID1 = 512
CAP = int(1.25 * BATCHES * SEQ / EXPERTS)
SLOTS = EXPERTS * CAP
SLOT_TILES = CAP // P
HALF_CAP = CAP // 2
LN_EPS = 1e-5
OUT_EPS = 1e-6
TOPW_EPS = 1e-6
TOP_BIT = 29
OUTSIDE = 2 * SLOTS

PROJECT_END = 0.3
MAXIMA_END = 0.65
MIX_START = 0.5

C_IDENT = 0
C_BEFORE = C_IDENT + P
C_LOWER = C_BEFORE + P
C_SLOT0 = C_LOWER + EXPERTS * EXPERTS
C_WIDTH = C_SLOT0 + EXPERTS


def constants():
    c = np.zeros((P, C_WIDTH), np.float32)
    c[:, C_IDENT:C_BEFORE] = np.eye(P)
    c[:, C_BEFORE:C_LOWER] = np.triu(np.ones((P, P)), 1)
    c[:, C_LOWER:C_SLOT0] = np.tril(np.ones((EXPERTS, EXPERTS)), -1).reshape(-1)
    c[:, C_SLOT0:] = np.arange(EXPERTS) * CAP
    return c


def merge(*streams):
    live = [[start, (end - start) / steps, g] for g, steps, start, end in streams]
    while live:
        live.sort(key=lambda x: x[0])
        first = live[0]
        if next(first[2], "end") == "end":
            live.remove(first)
        else:
            first[0] += first[1]


def build(nc, x, w_qkv0, w_out0, b_out0, gamma0, beta0, gate0, up0, down0, bias0,
          w_qkv1, b_qk1, b_v1, w_out1, b_out1, router1, wg1, wu1, wd1, consts, out,
          batches=BATCHES, stages=6):
    fp32 = mybir.dt.float32
    f32r = mybir.dt.float32r
    i32 = mybir.dt.int32
    u32 = mybir.dt.uint32
    ALU = mybir.AluOpType
    ACT = mybir.ActivationFunctionType
    AX = mybir.AxisListType

    ctx = ExitStack()
    with ctx:
        def sb(name, shape, dt=fp32):
            return ctx.enter_context(nc.sbuf_tensor(name, shape, dt))

        def sem(name):
            return ctx.enter_context(nc.semaphore(name))

        class Queue:

            def __init__(self, name):
                self.done = sem(f"{name}_done")
                self.count = 0
                self.steps = []

            def __call__(self, emit, *tickets, signal=True):
                if signal:
                    self.count += 1
                self.steps.append((emit, tickets, self.done if signal else None, 1))
                return (self.done, self.count) if signal else None

            def transfer(self, emit, arrival, *tickets):
                arrival.count += 16
                self.steps.append((emit, tickets, arrival.sem, 16))
                return (arrival.sem, arrival.count)

            def run(self, eng):
                waited = {}
                for emit, tickets, counter, by in self.steps:
                    for t in tickets:
                        if t is None:
                            continue
                        s, value = t
                        if waited.get(s.name, 0) < value:
                            eng.wait_ge(s, value)
                            waited[s.name] = value
                    ins = emit()
                    if counter is not None:
                        ins.then_inc(counter, by)

        class Arrival:

            def __init__(self, name):
                self.sem = sem(name)
                self.count = 0

            @property
            def all(self):
                return (self.sem, self.count)

        class Place:

            def __init__(self, ap):
                self.ap = ap
                self.release(())

            def release(self, tickets):
                self.tickets = tickets
                self.in_use = False

            free = property(lambda self: self.tickets, release)

        class Ring:
            def __init__(self, aps):
                self.places = [Place(a) for a in aps]

            def take(self):
                place = next(p for p in self.places if not p.in_use)
                self.places.remove(place)
                self.places.append(place)
                place.in_use = True
                return place

        pe, act, dve, pool, sp = (Queue(n) for n in ("pe", "act", "dve", "pool", "sp"))
        T_, S_, V_, G_, Y_ = nc.tensor, nc.scalar, nc.vector, nc.gpsimd, nc.sync

        X = sb("X", [P, TILES, DIM])
        cst = sb("cst", [P, C_WIDTH])
        ident = cst[:, C_IDENT:C_BEFORE]
        before = cst[:, C_BEFORE:C_LOWER]
        lower = cst[:, C_LOWER:C_SLOT0].rearrange("p (a e j) -> p a e j", a=1, e=EXPERTS)
        slot0 = cst[:, C_SLOT0:C_WIDTH].rearrange("p (a e) -> p a e", a=1)
        ones = sb("ones", [P, P])
        minus_half = sb("minus_half", [P, TILES_B])

        wqkv = sb("wqkv", [P, 3 * INNER])
        wout = sb("wout", [P, GROUPS, DIM])
        bqk = sb("bqk", [P, 2 * GROUPS])
        bv = sb("bv", [P, GROUPS])
        rows = sb("rows", [P, 4, DIM])
        gate_w = sb("gate_w", [P, EXPERTS])
        gate_b = sb("gate_b", [P, EXPERTS])
        router_w = sb("router_w", [P, EXPERTS])

        xn = [sb(f"xn{i}", [P, TILES_B, DIM]) for i in range(2)]
        xT = Ring([sb(f"xT{i}", [P, SEQ])[:, :] for i in range(2)])
        stats = [sb(f"stats{i}", [P, TILES_B, 6]) for i in range(2)]
        mv = [sb(f"mv{i}", [P, TILES_B, 2]) for i in range(2)]
        rstd = [sb(f"rstd{i}", [P, TILES_B]) for i in range(2)]

        ARENA = 82 * 256
        arena = sb("arena", [P, ARENA])

        class Carve:
            def __init__(self):
                self.at = 0

            def __call__(self, *shape):
                n = int(np.prod(shape))
                ap = arena[:, self.at:self.at + n]
                self.at += n
                assert self.at <= ARENA, self.at
                if len(shape) == 1:
                    return ap
                names = " ".join("abcd"[:len(shape)])
                return ap.rearrange(f"p ({names}) -> p {names}", **dict(zip("abcd", shape)))

        psum = ctx.enter_context(nc.psum_tensor("psum", [P, 8, 512], fp32))
        bank = [psum[:, i, :] for i in range(8)]
        banks_a = Ring(bank[0:2])
        banks_b = Ring(bank[2:5])
        banks_m = Ring(bank[6:8])

        slots_in = nc.dram_tensor("slots_in", (SLOTS, DIM), fp32, kind="Internal").ap()
        slots_out = nc.dram_tensor("slots_out", (SLOTS, DIM), fp32, kind="Internal").ap()

        got_x = [Arrival(f"got_x{b}") for b in range(2)]
        got_w = Arrival("got_w")
        got_w2 = Arrival("got_w2")
        got_small = Arrival("got_small")
        x_v = x.rearrange("b (t p) d -> b p t d", p=P)
        out_v = out.rearrange("b (t p) d -> b p t d", p=P)

        def load(dst, src, arrival, *tickets):
            return sp.transfer(lambda: Y_.dma_start(dst, src), arrival, *tickets)

        in_consts = load(cst[:, :], consts, Arrival("got_consts"))
        load(X[:, 0:TILES_B, :], x_v[0], got_x[0])
        first_batch = got_x[0].all
        for r, v in enumerate((b_out0, gamma0, beta0, b_out1)):
            load(rows[:, r, :], v.partition_broadcast(P), got_small)
        load(gate_b[:, :], bias0.partition_broadcast(P), got_small)
        load(gate_w[:, :], gate0, got_small)
        load(router_w[:, :], router1, got_small)
        load(bqk[:, :], b_qk1, got_small)
        load(bv[:, :], b_v1, got_small)
        small = got_small.all

        t_ones = dve(lambda: V_.memset(ones[:, :], 1.0))
        t_mh = dve(lambda: V_.memset(minus_half[:, :], -0.5))

        x_ready = [None] * batches

        class Norm:

            def __init__(self):
                self.n = 0
                self.xn_free = [(), ()]
                self.last = [None, None]

        norm_state = Norm()

        def moments(src_tiles, which, eps, *tickets):
            st, m, r = stats[which], mv[which], rstd[which]
            prev = norm_state.last[which]
            ts = []
            for t in range(TILES_B):
                ts.append(dve(lambda t=t: V_.bn_stats(st[:, t, :], src_tiles[t]), *tickets, prev))
            for t in range(TILES_B):
                last = dve(lambda t=t: V_.bn_aggr(m[:, t, :], st[:, t, :]), ts[t], prev)
            var = dve(lambda: V_.tensor_scalar(r[:, :], m[:, :, 1], eps, None, ALU.add), last, prev)
            root = pool(lambda: G_.tensor_tensor(r[:, :], r[:, :], minus_half[:, :], ALU.pow),
                        var, t_mh)
            return root

        def normalise(b, keep_rows=None):
            w = norm_state.n % 2
            norm_state.n += 1
            src = [X[:, b * TILES_B + t, :] for t in range(TILES_B)]
            root = moments(src, w, LN_EPS, x_ready[b])
            yield
            dst = xn[w][:, :, :] if keep_rows is None else keep_rows
            for t in range(TILES_B):
                normed = dve(lambda t=t: V_.tensor_scalar(dst[:, t, :], src[t], mv[w][:, t, 0:1],
                                                          rstd[w][:, t:t + 1], ALU.subtract, ALU.mult),
                             root, *norm_state.xn_free[w])
            norm_state.last[w] = normed
            yield
            bk = banks_m.take()
            for t in range(TILES_B):
                turned = pe(lambda t=t: T_.matmul(bk.ap[:, t * P:(t + 1) * P], dst[:, t, :], ident,
                                                  is_transpose=True),
                            normed, in_consts, *bk.free, signal=t == TILES_B - 1)
            norm_state.xn_free[w] = (turned,)
            place = xT.take()
            place.ready = act(lambda: S_.activation(place.ap, bk.ap, ACT.Copy), turned, *place.free)
            place.normed = normed
            bk.free = (place.ready,)
            normalise.place = place
            yield

        def drain(gen):
            for _ in gen:
                pass

        beats = sb("beats", [P, TILES_B, EXPERTS, EXPERTS])
        equal = sb("equal", [P, TILES_B, EXPERTS, EXPERTS])

        gate_last = [None]

        def ranks(value, rank, *tickets):
            vj = value.unsqueeze(2).to_broadcast([P, TILES_B, EXPERTS, EXPERTS])
            ve = value.unsqueeze(3).to_broadcast([P, TILES_B, EXPERTS, EXPERTS])
            low = lower.to_broadcast([P, TILES_B, EXPERTS, EXPERTS])
            a = dve(lambda: V_.tensor_tensor(beats[:, :, :, :], vj, ve, ALU.is_gt),
                    gate_last[0], *tickets)
            c = dve(lambda: V_.tensor_tensor(equal[:, :, :, :], vj, ve, ALU.is_equal), gate_last[0])
            c = dve(lambda: V_.tensor_tensor(equal[:, :, :, :], equal[:, :, :, :], low, ALU.mult),
                    c, in_consts)
            c = dve(lambda: V_.tensor_tensor(beats[:, :, :, :], beats[:, :, :, :],
                                             equal[:, :, :, :], ALU.add), a, c)
            c = dve(lambda: V_.tensor_reduce(rank, beats[:, :, :, :], AX.X, ALU.add), c)
            gate_last[0] = c
            return c

        gates = {n: [sb(f"{n}{i}", [P, TILES_B, EXPERTS]) for i in range(2)]
                 for n in ("score", "value", "rank", "weight")}
        gate_free = [(), ()]

        def logits(place, weights):
            bk = banks_m.take()
            for t in range(TILES_B):
                done = pe(lambda t=t: T_.matmul(bk.ap[:, t * EXPERTS:(t + 1) * EXPERTS],
                                                place.ap[:, t * P:(t + 1) * P], weights,
                                                start=True, stop=True),
                          place.ready, small, *bk.free, signal=t == TILES_B - 1)
            view = bk.ap[:, 0:TILES_B * EXPERTS].rearrange("p (t e) -> p t e", t=TILES_B)
            return bk, view, done

        def experts0(carve_free):
            carve = Carve()
            up = carve(EXPERTS * HID0)
            down = carve(EXPERTS, 2, DIM)
            hid = Ring([carve(2, SEQ) for _ in range(3)])
            w_up = load(up, up0, got_w, *carve_free)
            w_down = load(down, down0.rearrange("p (e c) d -> p e c d", e=EXPERTS), got_w2, *carve_free)
            gate = {}

            def prepare(b):
                yield from normalise(b)
                place = normalise.place
                g = b % 2
                score, value, rank, weight = (gates[n][g] for n in ("score", "value", "rank", "weight"))
                bk, view, done = logits(place, gate_w[:, :])
                yield
                s = act(lambda: S_.activation(score[:, :, :], view, ACT.Sigmoid), done, *gate_free[g])
                bk.free = (s,)
                bias = gate_b[:, :].unsqueeze(1).to_broadcast([P, TILES_B, EXPERTS])
                v = dve(lambda: V_.tensor_tensor(value[:, :, :], score[:, :, :], bias, ALU.add),
                        s, small, *gate_free[g])
                yield
                r = ranks(value[:, :, :], rank[:, :, :], v)
                yield
                v = dve(lambda: V_.scalar_tensor_tensor(out=value[:, :, :], in0=rank[:, :, :],
                                                        scalar=float(TOP_K), in1=score[:, :, :],
                                                        op0=ALU.is_lt, op1=ALU.mult), r)
                w = dve(lambda: V_.scalar_tensor_tensor(out=weight[:, :, :], in0=value[:, :, :],
                                                        scalar=0.5, in1=value[:, :, :],
                                                        op0=ALU.mult, op1=ALU.mult), v)
                gate[b] = (place, weight, w)
                yield

            def compute(b):
                place, weight, w = gate[b]
                steps = []

                def up_step(e):
                    h = hid.take()
                    squares = []
                    for c in range(2):
                        bk = banks_a.take()
                        col = (e * 2 + c) * P
                        u = pe(lambda bk=bk, col=col: T_.matmul(bk.ap, up[:, col:col + P], place.ap,
                                                                start=True, stop=True),
                               w_up, place.ready, *bk.free)
                        r = dve(lambda bk=bk, h=h, c=c: V_.tensor_scalar(h.ap[:, c, :], bk.ap, 0.0, None,
                                                                         ALU.max), u, *h.free)
                        bk.free = (r,)
                        squares.append(act(lambda h=h, c=c: S_.activation(h.ap[:, c, :], h.ap[:, c, :],
                                                                          ACT.Square), r))
                    if e == EXPERTS - 1:
                        place.free = (u,)
                    steps.append((h, squares))

                def down_step(e):
                    h, squares = steps[e]
                    bk = banks_b.take()
                    for t in range(TILES_B):
                        for c in range(2):
                            d = pe(lambda t=t, c=c: T_.matmul(bk.ap[:, t * P:(t + 1) * P],
                                                              h.ap[:, c, t * P:(t + 1) * P],
                                                              down[:, e, c, :],
                                                              start=c == 0, stop=c == 1),
                                   *squares, w_down, *bk.free, signal=t == TILES_B - 1 and c == 1)
                    h.free = (d,)
                    for t in range(TILES_B):
                        tile = b * TILES_B + t
                        a = dve(lambda t=t, tile=tile: V_.scalar_tensor_tensor(
                            out=X[:, tile, :], in0=bk.ap[:, t * P:(t + 1) * P],
                            scalar=weight[:, t, e:e + 1], in1=X[:, tile, :],
                            op0=ALU.mult, op1=ALU.add), d, w, x_ready[b])
                    bk.free = (a,)
                    x_ready[b] = a
                    return a

                up_step(0)
                yield
                for e in range(EXPERTS):
                    if e + 1 < EXPERTS:
                        up_step(e + 1)
                        yield
                    last = down_step(e)
                    yield
                gate_free[b % 2] = (last,)

            if x_ready[0] is None:
                x_ready[0] = first_batch
                for b in range(1, batches):
                    x_ready[b] = load(X[:, b * TILES_B:(b + 1) * TILES_B, :], x_v[b], Arrival(f"got_xb{b}"))
            drain(prepare(0))
            for b in range(batches):
                more = [(prepare(b + 1), 6, 0, 1)] if b + 1 < batches else []
                merge((compute(b), 16, 0, 1), *more)
            return (x_ready[batches - 1], (pe.done, pe.count), (dve.done, dve.count), (act.done, act.count))

        QH, QL, KH, KL = range(4)
        halves = [sb(f"halves{i}", [P, 4, SEQ], f32r) for i in range(2)]
        halves_free = [(), ()]
        N_STACK = 3
        stack = [sb(f"stack{i}", [P, 2, 4, SEQ], f32r) for i in range(N_STACK)]
        stack_free = [()] * N_STACK
        stacked = [Arrival(f"stacked{i}") for i in range(N_STACK)]
        max_rows = [Arrival(f"max_rows{i}") for i in range(N_STACK)]
        N_VALUES = 4
        values = [sb(f"values{i}", [P, TILES_B, P]) for i in range(N_VALUES)]
        values_free = [()] * N_VALUES
        top = [sb(f"top{i}", [P, 16]) for i in range(2)]
        top_free = [(), ()]
        mh = [sb(f"mh{i}", [16, P], f32r) for i in range(2)]
        ml = [sb(f"ml{i}", [16, P], f32r) for i in range(2)]
        m_free = [(), ()]
        bank_s = Ring(bank[0:2])
        bank_t = Ring(bank[2:4])
        bank_o = Ring(bank[4:6])

        def attention(wqkv_src, wout_src, heads, width, bias_qk, finish, region_free):
            scale = float(width) ** -0.5
            if heads == 4:
                copies = ((0, 0, QH, KH), (32, 0, QL, KH), (64, 0, QH, KL))
                parts = ((96, 98, 0),)
            else:
                copies = ((0, 0, QH, KH), (64, 0, QL, KH), (0, 2, QH, KL))
                parts = ((P, P, 0), (64, 66, 2))
            max_at, max_slot = parts[-1][0], parts[-1][2]
            carve = Carve()
            prob = Ring([carve(heads, SEQ) for _ in range(5)])
            pair = Ring([carve(heads, SEQ) for _ in range(3)])
            inv = Ring([carve(SEQ) for _ in range(1)])
            mixed = carve(GROUPS, SEQ)
            mixed_free = [()]
            load(wqkv[:, :], wqkv_src, got_w, *region_free)
            load(wout[:, :, :], wout_src, got_w, *region_free)
            t_w = got_w.all
            t_ones_rows = [dve(lambda s=s: V_.memset(
                s[max_at:max_at + 2, 1, max_slot:max_slot + heads, :].bitcast(fp32), 1.0), *region_free)
                for s in stack]
            places, info = {}, {}

            def project(b, g, n):
                hv, st, i, s = halves[n % 2], stack[n % N_STACK], n % 2, n % N_STACK
                place = places[b]
                hf = halves_free[i]
                split = []
                for which, hi, lo in ((0, QH, QL), (1, KH, KL)):
                    bk = banks_m.take()
                    col = which * INNER + g * P
                    p_ = pe(lambda bk=bk, col=col: T_.matmul(bk.ap, wqkv[:, col:col + P], place.ap,
                                                             start=True, stop=True),
                            t_w, place.ready, *bk.free)
                    if bias_qk:
                        bias = bqk[:, which * GROUPS + g:which * GROUPS + g + 1]
                        h_ = act(lambda bk=bk, hi=hi, bias=bias: S_.activation(
                            hv[:, hi, :], bk.ap, ACT.Identity, bias=bias), p_, small, *hf)
                        l_ = dve(lambda bk=bk, hi=hi, lo=lo, bias=bias: V_.scalar_tensor_tensor(
                            out=hv[:, lo, :], in0=bk.ap, scalar=bias, in1=hv[:, hi, :].bitcast(fp32),
                            op0=ALU.add, op1=ALU.subtract), h_, *hf)
                    else:
                        h_ = act(lambda bk=bk, hi=hi: S_.activation(hv[:, hi, :], bk.ap, ACT.Copy), p_, *hf)
                        l_ = dve(lambda bk=bk, hi=hi, lo=lo: V_.tensor_tensor(
                            hv[:, lo, :], bk.ap, hv[:, hi, :].bitcast(fp32), ALU.subtract), h_, *hf)
                    bk.free = (l_,)
                    split += [h_, l_]
                    yield
                for at, slot, q_part, k_part in copies:
                    for h in range(heads):
                        sp.transfer(lambda at=at, slot=slot, q_part=q_part, k_part=k_part, h=h: Y_.dma_start(
                            st[at:at + width, :, slot + h, :].bitcast(fp32),
                            hv[width * h:width * (h + 1), q_part:k_part + 1:k_part - q_part, :].bitcast(fp32)),
                            stacked[s], *split, *stack_free[s])
                halves_free[i] = (stacked[s].all,)
                bk = banks_m.take()
                for t in range(TILES_B):
                    p_ = pe(lambda t=t, bk=bk: T_.matmul(bk.ap[:, t * P:(t + 1) * P],
                                                         place.ap[:, t * P:(t + 1) * P],
                                                         wqkv[:, 2 * INNER + g * P:2 * INNER + (g + 1) * P],
                                                         start=True, stop=True),
                            t_w, place.ready, *bk.free, signal=t == TILES_B - 1)
                if g == GROUPS - 1:
                    place.free = (p_,)
                v_ = act(lambda bk=bk: S_.activation(values[n % N_VALUES][:, :, :], bk.ap.rearrange(
                    "p (t f) -> p t f", t=TILES_B), ACT.Copy), p_, *values_free[n % N_VALUES])
                bk.free = (v_,)
                info[n] = dict(stacked=stacked[s].all, values=v_)
                yield

            def product(bk, st, side, h, cols, with_max, *tickets):
                for r, (plain, full, slot) in enumerate(parts):
                    k = full if with_max else plain
                    last = r == len(parts) - 1
                    done = pe(lambda k=k, slot=slot, r=r, last=last: T_.matmul(
                        bk.ap, st[0:k, side, slot + h, cols], st[0:k, 1 - side, slot + h, :],
                        start=r == 0, stop=last), *tickets, *bk.free, signal=last)
                return done

            def maxima(b, g, n):
                st, i, s = stack[n % N_STACK], n % 2, n % N_STACK
                d = info[n]
                for h in range(heads):
                    for qt in range(TILES_B):
                        bk = bank_s.take()
                        s_ = product(bk, st, 0, h, slice(qt * P, (qt + 1) * P), False, d["stacked"])
                        m_ = dve(lambda bk=bk, h=h, qt=qt: V_.reduce_max(
                            top[i][:, h * TILES_B + qt:h * TILES_B + qt + 1], bk.ap, AX.X),
                            s_, *top_free[i])
                        bk.free = (m_,)
                        yield
                n_top = heads * TILES_B
                bk = banks_m.take()
                t_ = pe(lambda bk=bk: T_.matmul(bk.ap[0:n_top, 0:P], top[i][:, 0:n_top], ident,
                                                is_transpose=True), m_, *bk.free)
                top_free[i] = (t_,)
                a_ = act(lambda bk=bk: S_.activation(mh[i][0:n_top, :], bk.ap[0:n_top, 0:P], ACT.Copy,
                                                     scale=-1.0), t_, *m_free[i])
                b_ = dve(lambda bk=bk: V_.scalar_tensor_tensor(
                    out=ml[i][0:n_top, :], in0=bk.ap[0:n_top, 0:P], scalar=-1.0,
                    in1=mh[i][0:n_top, :].bitcast(fp32), op0=ALU.mult, op1=ALU.subtract),
                    a_, *m_free[i])
                bk.free = (b_,)
                for r, part in enumerate((mh[i], ml[i])):
                    sp.transfer(lambda r=r, part=part: Y_.dma_start(
                        st[max_at + r:max_at + r + 1, 0, max_slot:max_slot + heads, :].rearrange(
                            "a h (t q) -> a (h t) q", t=TILES_B).bitcast(fp32),
                        part[0:n_top, :].bitcast(fp32)), max_rows[s], a_, b_)
                m_free[i] = (max_rows[s].all,)
                d["max_rows"] = max_rows[s].all
                yield

            def weigh(n, kt):
                d = info[n]
                pr, e_ = d["prob"][kt]
                for h in range(heads):
                    c = slice(width * h, width * (h + 1))
                    v_ = pe(lambda c=c, h=h: T_.matmul(
                        d["o"].ap[c, :], values[n % N_VALUES][:, kt, c], pr.ap[:, h, :],
                        start=kt == 0, stop=kt == TILES_B - 1, tile_position=(0, width * h)),
                        e_, d["values"], *d["o"].free, signal=h == heads - 1)
                d["weighed"] = v_
                if kt % 2:
                    pr.free = (v_, d["sum"][kt // 2])
                    d["prob"][kt - 1][0].free = (d["even"], d["sum"][kt // 2])
                else:
                    d["even"] = v_

            def probabilities(b, g, n):
                st, s = stack[n % N_STACK], n % N_STACK
                d = info[n]
                d["prob"], d["pair"], d["sum"] = [], [], []
                d["o"] = bank_o.take()
                for kt in range(TILES_B):
                    pr = prob.take()
                    for h in range(heads):
                        bk = bank_t.take()
                        s_ = product(bk, st, 1, h, slice(kt * P, (kt + 1) * P), True,
                                     d["stacked"], d["max_rows"], t_ones_rows[s])
                        e_ = act(lambda bk=bk, pr=pr, h=h: S_.activation(pr.ap[:, h, :], bk.ap, ACT.Exp,
                                                                         scale=scale), s_, *pr.free)
                        bk.free = (e_,)
                        yield
                    d["prob"].append((pr, e_))
                    if kt % 2:
                        two = pair.take()
                        p0, p1 = d["prob"][kt - 1][0], pr
                        a_ = pool(lambda two=two, p0=p0, p1=p1: G_.tensor_tensor(two.ap, p0.ap, p1.ap,
                                                                                 ALU.add),
                                  e_, *two.free)
                        d["pair"].append((two, a_))
                        d["sum"].append(a_)
                    if kt:
                        weigh(n, kt - 1)
                        yield
                stack_free[s] = (s_,)

            def last_tile(n):
                weigh(n, TILES_B - 1)
                values_free[n % N_VALUES] = (info[n]["weighed"],)
                yield

            def mix(b, g, n):
                d = info.pop(n)
                dn = banks_m.take()
                for j, (two, a_) in enumerate(d["pair"]):
                    for h in range(heads):
                        c = slice(width * h, width * (h + 1))
                        n_ = pe(lambda j=j, c=c, two=two, h=h: T_.matmul(
                            dn.ap[c, :], ones[:, 0:width], two.ap[:, h, :],
                            start=j == 0, stop=j == len(d["pair"]) - 1, tile_position=(0, width * h)),
                            a_, t_ones, *dn.free, signal=h == heads - 1)
                    two.free = (n_,)
                    yield
                r = inv.take()
                for q in range(TILES_B):
                    c = slice(q * P, (q + 1) * P)
                    r_ = dve(lambda c=c: V_.reciprocal(r.ap[:, c], dn.ap[:, c]), n_, *r.free)
                    yield
                dn.free = (r_,)
                o = d["o"]
                o_ = dve(lambda: V_.tensor_tensor(mixed[:, g, :], o.ap, r.ap, ALU.mult),
                         d["weighed"], r_, *mixed_free[0])
                o.free = (o_,)
                r.free = (o_,)
                if bias_qk:
                    o_ = dve(lambda: V_.tensor_scalar(mixed[:, g, :], mixed[:, g, :], bv[:, g:g + 1],
                                                      None, ALU.add), o_, small)
                d_mixed[0] = o_
                yield

            d_mixed = [None]

            def project_out(b):
                bk = banks_m.take()
                for t in range(TILES_B):
                    for gg in range(GROUPS):
                        p_ = pe(lambda t=t, gg=gg: T_.matmul(bk.ap[:, t * P:(t + 1) * P],
                                                             mixed[:, gg, t * P:(t + 1) * P],
                                                             wout[:, gg, :],
                                                             start=gg == 0, stop=gg == GROUPS - 1),
                                d_mixed[0], t_w, *bk.free,
                                signal=t == TILES_B - 1 and gg == GROUPS - 1)
                        if gg % 4 == 3:
                            yield
                mixed_free[0] = (p_,)
                yield from finish(b, bk, p_)

            order = [(b, g) for b in range(batches) for g in range(GROUPS)]
            drain(normalise(0))
            places[0] = normalise.place
            for n in range(len(order) + 4):
                streams = []
                if 0 <= n - 3 < len(order):
                    streams.append((last_tile(n - 3), 1, 0, 0))
                if n < len(order):
                    b, g = order[n]
                    streams.append((project(b, g, n), 3, 0, PROJECT_END))
                if 0 <= n - 1 < len(order):
                    streams.append((maxima(*order[n - 1], n - 1), heads * TILES_B, 0, MAXIMA_END))
                if 0 <= n - 2 < len(order):
                    streams.append((probabilities(*order[n - 2], n - 2), (heads + 1) * TILES_B, 0, 1))
                if 0 <= n - 3 < len(order):
                    streams.append((mix(*order[n - 3], n - 3), 7, MIX_START, 1))
                if n - 4 >= 0 and order[n - 4][1] == GROUPS - 1:
                    streams.append((project_out(order[n - 4][0]), 12, 0, 0.9 * MIX_START))
                if n < len(order) and g == GROUPS - 2 and b + 1 < batches:
                    def ahead(b=b):
                        yield from normalise(b + 1)
                        places[b + 1] = normalise.place
                    streams.append((ahead(), 3, MIX_START, 1))
                merge(*streams)
            return ((pe.done, pe.count), (dve.done, dve.count), (act.done, act.count),
                    (pool.done, pool.count), *(a.all for a in stacked), *(a.all for a in max_rows))

        y = [sb("y", [P, TILES_B, DIM])]
        y_free = [()]

        def row(r):
            return rows[:, r, :].unsqueeze(1).to_broadcast([P, TILES_B, DIM])

        def finish0(b, bk, p_):
            i = 0
            view = bk.ap.rearrange("p (t d) -> p t d", t=TILES_B)
            a = dve(lambda: V_.tensor_tensor(y[i][:, :, :], view, row(0), ALU.add), p_, small, *y_free[i])
            bk.free = (a,)
            yield
            w = norm_state.n % 2
            norm_state.n += 1
            root = moments([y[i][:, t, :] for t in range(TILES_B)], w, OUT_EPS, a)
            yield
            for t in range(TILES_B):
                a = dve(lambda t=t: V_.tensor_scalar(y[i][:, t, :], y[i][:, t, :], mv[w][:, t, 0:1],
                                                     rstd[w][:, t:t + 1], ALU.subtract, ALU.mult), root)
            norm_state.last[w] = a
            yield
            a = dve(lambda: V_.tensor_tensor(y[i][:, :, :], y[i][:, :, :], row(1), ALU.mult), a)
            a = dve(lambda: V_.tensor_tensor(y[i][:, :, :], y[i][:, :, :], row(2), ALU.add), a)
            xb = X[:, b * TILES_B:(b + 1) * TILES_B, :]
            a = dve(lambda: V_.tensor_tensor(xb, xb, y[i][:, :, :], ALU.add), a, x_ready[b])
            y_free[i] = (a,)
            x_ready[b] = a
            yield

        def finish1(b, bk, p_):
            i = 0
            view = bk.ap.rearrange("p (t d) -> p t d", t=TILES_B)
            a = dve(lambda: V_.tensor_tensor(y[i][:, :, :], view, row(3), ALU.add), p_, small, *y_free[i])
            bk.free = (a,)
            xb = X[:, b * TILES_B:(b + 1) * TILES_B, :]
            a = dve(lambda: V_.tensor_tensor(xb, xb, y[i][:, :, :], ALU.add), a, x_ready[b])
            y_free[i] = (a,)
            x_ready[b] = a
            yield

        gathered = [Arrival(f"gathered{i}") for i in range(4)]
        scattered = Arrival("scattered")
        zeroed = Arrival("zeroed")
        slots_loaded = [Arrival(f"slots_loaded{i}") for i in range(2)]
        slots_stored = [Arrival(f"slots_stored{i}") for i in range(2)]
        dram_free = [()]
        tiles = batches * TILES_B

        def experts1(region_free):
            carve = Carve()
            wg, wu, wd = (wqkv[:, i * 2 * HID1:(i + 1) * 2 * HID1].rearrange("p (e f) -> p e f", e=2)
                          for i in range(3))
            wd = wd.rearrange("p e (f d) -> p e f d", d=DIM)
            XN = carve(TILES, DIM)
            W = carve(tiles, EXPERTS)
            R = carve(tiles, EXPERTS)
            ge = carve(tiles, EXPERTS)
            flags = carve(2, tiles, EXPERTS)
            scan = [carve(2, tiles, EXPERTS) for _ in range(2)]
            tmp = [carve(tiles, EXPERTS) for _ in range(3)]
            cnt = carve(EXPERTS)
            thr, cand, step = (carve(EXPERTS) for _ in range(3))
            slot_k = carve(2, tiles)
            kept_k = carve(2, tiles)
            w_k = carve(2, tiles)
            idx_out = carve(2, tiles)
            idx_in = carve(2, tiles)
            dst_t = Ring([carve(CAP) for _ in range(2)])
            rows_in = [carve(SLOT_TILES, DIM) for _ in range(2)]
            rows_free = [(), ()]
            sig = Ring([carve(HALF_CAP) for _ in range(3)])
            hid = Ring([carve(HID1 // P, CAP) for _ in range(1)])
            eo = Ring([carve(SLOT_TILES, DIM) for _ in range(2)])
            got = [carve(DIM) for _ in range(8)]
            got_free = [()] * 8
            soft = [carve(TILES_B) for _ in range(4)]

            t_wt = {}
            wt_free = [()] * 2

            def load_weights(e):
                i = e % 2
                a = Arrival(f"we{len(we_sems)}") if len(we_sems) < 2 else we_sems[i]
                if len(we_sems) < 2:
                    we_sems.append(a)
                waits = (*region_free, *wt_free[i])
                load(wg[:, i, :], wg1[:, e, :], a, *waits)
                load(wu[:, i, :], wu1[:, e, :], a, *waits)
                load(wd[:, i, :, :], wd1[:, e, :, :], a, *waits)
                t_wt[e] = a.all

            for e in range(2):
                load_weights(e)

            soft_free = [None]

            def route(b):
                yield from normalise(b, XN[:, b * TILES_B:(b + 1) * TILES_B, :])
                place = normalise.place
                g = b % 2
                score, value = (gates[n][g] for n in ("score", "value"))
                bk, view, done = logits(place, router_w[:, :])
                place.free = (done,)
                yield
                here = slice(b * TILES_B, (b + 1) * TILES_B)
                wide = [P, TILES_B, EXPERTS]
                top_, sum_, sel_, inv_ = soft
                f = soft_free[0]
                a = dve(lambda: V_.tensor_reduce(top_, view, AX.X, ALU.max), done, f)
                a = dve(lambda: V_.tensor_tensor(value[:, :, :], view, top_.unsqueeze(2).to_broadcast(wide),
                                                 ALU.subtract), a, *gate_free[g])
                bk.free = (a,)
                e_ = act(lambda: S_.activation(score[:, :, :], value[:, :, :], ACT.Exp), a)
                a = dve(lambda: V_.tensor_reduce(sum_, score[:, :, :], AX.X, ALU.add), e_, f)
                a = dve(lambda: V_.reciprocal(inv_, sum_), a)
                a = dve(lambda: V_.tensor_tensor(score[:, :, :], score[:, :, :],
                                                 inv_.unsqueeze(2).to_broadcast(wide), ALU.mult), a)
                yield
                a = ranks(score[:, :, :], R[:, here, :], a, *region_free)
                a = dve(lambda: V_.scalar_tensor_tensor(out=value[:, :, :], in0=R[:, here, :],
                                                        scalar=float(TOP_K), in1=score[:, :, :],
                                                        op0=ALU.is_lt, op1=ALU.mult), a)
                a = dve(lambda: V_.tensor_reduce(sel_, value[:, :, :], AX.X, ALU.add), a)
                a = dve(lambda: V_.tensor_scalar(sel_, sel_, TOPW_EPS, None, ALU.add), a)
                a = dve(lambda: V_.reciprocal(inv_, sel_), a)
                a = dve(lambda: V_.tensor_tensor(W[:, here, :], value[:, :, :],
                                                 inv_.unsqueeze(2).to_broadcast(wide), ALU.mult), a)
                soft_free[0] = a
                gate_free[g] = (a,)
                yield
                route.last = a

            for b in range(batches):
                drain(route(b))
            a = route.last

            def bits(v):
                return v.bitcast(i32)

            wide = [P, tiles, EXPERTS]
            a = dve(lambda: V_.memset(bits(thr), 0), a)
            for bit in range(TOP_BIT, -1, -1):
                a = dve(lambda bit=bit: V_.tensor_scalar(bits(cand), bits(thr), 1 << bit, None,
                                                         ALU.bitwise_or), a)
                a = dve(lambda: V_.tensor_tensor(ge, W, cand.unsqueeze(1).to_broadcast(wide),
                                                 ALU.is_ge), a)
                a = dve(lambda: V_.tensor_reduce(cnt, ge.rearrange("p t e -> p e t"), AX.X, ALU.add), a)
                bk = banks_m.take()
                c_ = pe(lambda bk=bk: T_.matmul(bk.ap[:, 0:EXPERTS], ones[:, :], cnt,
                                                start=True, stop=True), a, t_ones, *bk.free)
                a = dve(lambda bk=bk, bit=bit: V_.tensor_scalar(bits(step), bk.ap[:, 0:EXPERTS],
                                                                float(CAP), float(1 << bit),
                                                                ALU.is_ge, ALU.mult), c_)
                bk.free = (a,)
                a = dve(lambda: V_.tensor_tensor(bits(thr), bits(thr), bits(step), ALU.bitwise_or), a)

            thr_b = thr.unsqueeze(1).to_broadcast(wide)
            over, tied = flags[:, 0], flags[:, 1]
            a0 = dve(lambda: V_.tensor_tensor(over, W, thr_b, ALU.is_gt), a)
            a = dve(lambda: V_.tensor_tensor(tied, W, thr_b, ALU.is_equal), a)
            a = dve(lambda: V_.scalar_tensor_tensor(out=tied, in0=W, scalar=0.0, in1=tied,
                                                    op0=ALU.is_gt, op1=ALU.mult), a)
            flat = "p a t e -> p (a t e)"
            inside, totals = banks_b.take(), banks_b.take()
            n_flags = 2 * tiles * EXPERTS
            i_ = pe(lambda: T_.matmul(inside.ap[:, 0:n_flags], before, flags.rearrange(flat),
                                      start=True, stop=True), a0, a, in_consts, *inside.free)
            t_ = pe(lambda: T_.matmul(totals.ap[:, 0:n_flags], ones[:, :], flags.rearrange(flat),
                                      start=True, stop=True), *totals.free)
            a = dve(lambda: V_.tensor_copy(scan[0].rearrange(flat), totals.ap[:, 0:n_flags]), t_)
            totals.free = (a,)
            s, shift = 0, 1
            while shift < tiles:
                src, dst = scan[s], scan[1 - s]
                b1 = dve(lambda src=src, dst=dst, k=shift: V_.tensor_tensor(
                    dst[:, :, k:, :], src[:, :, k:, :], src[:, :, :tiles - k, :], ALU.add), a)
                a = dve(lambda src=src, dst=dst, k=shift: V_.tensor_copy(
                    dst[:, :, :k, :], src[:, :, :k, :]), b1)
                s, shift = 1 - s, shift * 2
            upto, pos = scan[s], scan[1 - s]
            a = dve(lambda: V_.tensor_copy(pos.rearrange(flat), inside.ap[:, 0:n_flags]), a, i_)
            inside.free = (a,)
            if tiles > 1:
                a = dve(lambda: V_.tensor_tensor(pos[:, :, 1:, :], pos[:, :, 1:, :],
                                                 upto[:, :, :tiles - 1, :], ALU.add), a)
            all_over = upto[:, 0, tiles - 1:tiles, :].to_broadcast(wide)
            pos_o, pos_t = pos[:, 0], pos[:, 1]
            a = dve(lambda: V_.tensor_tensor(pos_t, pos_t, all_over, ALU.add), a)
            a = dve(lambda: V_.scalar_tensor_tensor(out=tied, in0=pos_t, scalar=float(CAP), in1=tied,
                                                    op0=ALU.is_lt, op1=ALU.mult), a)
            m0, m1, m2 = tmp
            kept = ge
            a = dve(lambda: V_.tensor_tensor(m0, over, pos_o, ALU.mult), a)
            a = dve(lambda: V_.tensor_tensor(m1, tied, pos_t, ALU.mult), a)
            a = dve(lambda: V_.tensor_tensor(m0, m0, m1, ALU.add), a)
            a = dve(lambda: V_.tensor_tensor(m0, m0, slot0.to_broadcast(wide), ALU.add), a)
            a = dve(lambda: V_.tensor_tensor(kept, over, tied, ALU.add), a)
            for k in range(TOP_K):
                a = dve(lambda k=k: V_.scalar_tensor_tensor(out=m1, in0=R, scalar=float(k), in1=kept,
                                                            op0=ALU.is_equal, op1=ALU.mult), a)
                a = dve(lambda k=k: V_.tensor_reduce(kept_k[:, k, :], m1, AX.X, ALU.add), a)
                a = dve(lambda k=k: V_.tensor_tensor(m2, m1, m0, ALU.mult), a)
                a = dve(lambda k=k: V_.tensor_reduce(slot_k[:, k, :], m2, AX.X, ALU.add), a)
                a = dve(lambda k=k: V_.tensor_tensor(m2, m1, W, ALU.mult), a)
                a = dve(lambda k=k: V_.tensor_reduce(w_k[:, k, :], m2, AX.X, ALU.add), a)
            a = dve(lambda: V_.tensor_scalar(w_k, w_k, 0.5, None, ALU.mult), a)
            a = dve(lambda: V_.tensor_copy(bits(idx_in), slot_k), a)
            a = dve(lambda: V_.tensor_scalar(kept_k, kept_k, -float(OUTSIDE), float(OUTSIDE),
                                             ALU.mult, ALU.add), a)
            a = dve(lambda: V_.tensor_tensor(bits(idx_out), slot_k, kept_k, ALU.add), a)
            t_idx = a

            for t in range(tiles):
                for k in range(TOP_K):
                    pool.transfer(lambda t=t, k=k: G_.indirect_dma_start(
                        slots_in, bass.IndirectOffsetOnAxis(ap=idx_out[:, k, t:t + 1].bitcast(u32), axis=0),
                        XN[:, t, :], None, bounds_check=SLOTS - 1, oob_is_err=False),
                        scattered, t_idx, zeroed.all, *dram_free[0])

            in_v = slots_in.rearrange("(e s p) d -> e p s d", e=EXPERTS, p=P)
            out_slots = slots_out.rearrange("(e s p) d -> e p s d", e=EXPERTS, p=P)

            def load_rows(e):
                i = e % 2
                return load(rows_in[i], in_v[e], slots_loaded[i], scattered.all, *rows_free[i])

            t_rows = {0: load_rows(0)}
            for e in range(EXPERTS):
                i, wi = e % 2, e % 2
                if e + 1 < EXPERTS:
                    t_rows[e + 1] = load_rows(e + 1)
                dT = dst_t.take()
                cps = []
                for part, (lo_, hi_) in enumerate(((0, 4), (4, SLOT_TILES))):
                    bk = banks_m.take()
                    for s_ in range(lo_, hi_):
                        c_ = pe(lambda bk=bk, s_=s_, lo_=lo_, i=i: T_.matmul(
                            bk.ap[:, (s_ - lo_) * P:(s_ - lo_ + 1) * P], rows_in[i][:, s_, :], ident,
                            is_transpose=True), t_rows[e], *bk.free, signal=s_ == hi_ - 1)
                    n = (hi_ - lo_) * P
                    cp = dve(lambda bk=bk, dT=dT, lo_=lo_, n=n: V_.tensor_copy(
                        dT.ap[:, lo_ * P:lo_ * P + n], bk.ap[:, 0:n]), c_, *dT.free)
                    bk.free = (cp,)
                    cps.append(cp)
                rows_free[i] = (c_,)
                h = hid.take()
                for f in range(HID1 // P):
                    for half in range(2):
                        cols = slice(half * HALF_CAP, (half + 1) * HALF_CAP)
                        gb, ub = banks_a.take(), banks_b.take()
                        g_ = pe(lambda gb=gb, f=f, cols=cols, dT=dT, wi=wi: T_.matmul(
                            gb.ap[:, 0:HALF_CAP], wg[:, wi, f * P:(f + 1) * P], dT.ap[:, cols],
                            start=True, stop=True), *cps, t_wt[e], *gb.free)
                        u_ = pe(lambda ub=ub, f=f, cols=cols, dT=dT, wi=wi: T_.matmul(
                            ub.ap[:, 0:HALF_CAP], wu[:, wi, f * P:(f + 1) * P], dT.ap[:, cols],
                            start=True, stop=True), *ub.free)
                        sg = sig.take()
                        s_ = act(lambda sg=sg, gb=gb: S_.activation(sg.ap, gb.ap[:, 0:HALF_CAP], ACT.Silu),
                                 g_, *sg.free)
                        gb.free = (s_,)
                        m_ = dve(lambda sg=sg, ub=ub, h=h, f=f, cols=cols: V_.tensor_tensor(
                            h.ap[:, f, cols], ub.ap[:, 0:HALF_CAP], sg.ap, ALU.mult), s_, u_, *h.free)
                        ub.free = (m_,)
                        sg.free = (m_,)
                dT.free = (u_,)
                o = eo.take()
                outs = []
                for part, (lo_, hi_) in enumerate(((0, 4), (4, SLOT_TILES))):
                    bk = banks_m.take()
                    for s_ in range(lo_, hi_):
                        for f in range(HID1 // P):
                            d_ = pe(lambda bk=bk, s_=s_, lo_=lo_, f=f, h=h, wi=wi: T_.matmul(
                                bk.ap[:, (s_ - lo_) * P:(s_ - lo_ + 1) * P],
                                h.ap[:, f, s_ * P:(s_ + 1) * P], wd[:, wi, f, :],
                                start=f == 0, stop=f == HID1 // P - 1), m_, *bk.free,
                                signal=s_ == hi_ - 1 and f == HID1 // P - 1)
                    n = (hi_ - lo_) * P
                    c_ = act(lambda bk=bk, o=o, lo_=lo_, hi_=hi_, n=n: S_.activation(
                        o.ap[:, lo_:hi_, :], bk.ap[:, 0:n].rearrange("p (s d) -> p s d", d=DIM), ACT.Copy),
                        d_, *o.free)
                    bk.free = (c_,)
                h.free = (d_,)
                wt_free[wi] = (d_,)
                o.free = (sp.transfer(lambda o=o, e=e: Y_.dma_start(out_slots[e], o.ap),
                                      slots_stored[i], c_),)
                if e + 2 < EXPERTS:
                    load_weights(e + 2)
            stored = (slots_stored[0].all, slots_stored[1].all)
            for t in range(tiles):
                b = t // TILES_B
                for k in range(TOP_K):
                    n = (t * TOP_K + k)
                    j = n % 8
                    r = gathered8[j]
                    g_ = pool.transfer(lambda t=t, k=k, j=j: G_.indirect_dma_start(
                        got[j], None, slots_out,
                        bass.IndirectOffsetOnAxis(ap=idx_in[:, k, t:t + 1].bitcast(u32), axis=0),
                        bounds_check=SLOTS - 1, oob_is_err=False), r, *stored, *got_free[j])
                    a = dve(lambda t=t, k=k, j=j: V_.scalar_tensor_tensor(
                        out=X[:, t, :], in0=got[j], scalar=w_k[:, k, t:t + 1], in1=X[:, t, :],
                        op0=ALU.mult, op1=ALU.add), g_, x_ready[b], a)
                    got_free[j] = (a,)
                x_ready[b] = a
            dram_free[0] = (a, t_rows[EXPERTS - 1], t_rows[EXPERTS - 2], *stored)
            return (a, (pe.done, pe.count), (act.done, act.count), scattered.all, *stored)

        we_sems = []
        gathered8 = [Arrival(f"gath{i}") for i in range(8)]

        zero_v = slots_in.rearrange("(n p) d -> p n d", p=P)
        zeros = sb("zeros", [P, DIM])
        t_z = dve(lambda: V_.memset(zeros[:, :], 0.0))
        act.transfer(lambda: S_.dma_start(zero_v, zeros[:, :].unsqueeze(1).to_broadcast(
            [P, SLOTS // P, DIM])), zeroed, t_z)

        free = ()
        if stages >= 1:
            free = experts0(free)
        if stages >= 2:
            free = attention(w_qkv0, w_out0, 4, 32, False, finish0, free)
        if stages >= 3:
            free = experts0(free)
        if stages >= 4:
            free = experts1(free)
        if stages >= 5:
            free = attention(w_qkv1, w_out1, 2, 64, True, finish1, free)
        if stages >= 6:
            free = experts1(free)
        stored = Arrival("stored")
        for b in range(batches):
            sp.transfer(lambda b=b: Y_.dma_start(out_v[b], X[:, b * TILES_B:(b + 1) * TILES_B, :]),
                        stored, x_ready[b])

        block = ctx.enter_context(nc.Block())

        @block.tensor
        def _(eng):
            pe.run(eng)

        @block.scalar
        def _(eng):
            act.run(eng)

        @block.vector
        def _(eng):
            dve.run(eng)

        @block.gpsimd
        def _(eng):
            pool.run(eng)

        @block.sync
        def _(eng):
            sp.run(eng)
            eng.wait_ge(stored.sem, stored.count)
            for a in (zeroed, scattered, *slots_stored):
                if a.count:
                    eng.wait_ge(a.sem, a.count)


def lay_out(inputs):
    f = {k: np.asarray(v) for k, v in inputs.items()}
    w1, b1 = f["L1_attn_W_qkv"], f["L1_attn_b_qkv"]
    a = {
        "x": f["L0_attn_x"],
        "w_qkv0": f["L0_attn_w_qkv"],
        "w_out0": f["L0_attn_w_out"].reshape(GROUPS, P, DIM).transpose(1, 0, 2),
        "b_out0": f["L0_attn_b_out"], "gamma0": f["L0_attn_ln_gamma"], "beta0": f["L0_attn_ln_beta"],
        "gate0": f["L0_ffn_gate_w"].T,
        "up0": f["L0_ffn_w_up"].transpose(2, 0, 1).reshape(DIM, EXPERTS * HID0),
        "down0": f["L0_ffn_w_down"].transpose(2, 0, 1).reshape(2, P, EXPERTS, DIM)
                  .transpose(1, 2, 0, 3).reshape(P, EXPERTS * 2, DIM),
        "bias0": f["L0_ffn_expert_bias"],
        "w_qkv1": w1,
        "b_qk1": b1[:2 * INNER].reshape(2 * GROUPS, P).T,
        "b_v1": b1[2 * INNER:].reshape(GROUPS, P).T,
        "w_out1": f["L1_attn_W_out"].reshape(GROUPS, P, DIM).transpose(1, 0, 2),
        "b_out1": f["L1_attn_b_out"],
        "router1": f["L1_ffn_router_w"].T,
        "wg1": f["L1_ffn_wg"].transpose(1, 0, 2),
        "wu1": f["L1_ffn_wu"].transpose(1, 0, 2),
        "wd1": f["L1_ffn_wd"].reshape(EXPERTS, HID1 // P, P, DIM).transpose(2, 0, 1, 3),
        "consts": constants(),
    }
    return {k: np.ascontiguousarray(v) for k, v in a.items()}


def kernel(**inputs):
    import concourse.bacc as _bacc
    from concourse.bass_utils import run_bass_kernel_spmd as _run

    nc = _bacc.Bacc("TRN2", target_bir_lowering=False, num_devices=1)
    arrays, args = {}, {}
    for name, a in lay_out(inputs).items():
        arrays[f"in_{name}"] = a
        args[name] = nc.dram_tensor(f"in_{name}", a.shape, mybir.dt.from_np(a.dtype),
                                    kind="ExternalInput").ap()
    out = nc.dram_tensor("out", (BATCHES, SEQ, DIM), mybir.dt.float32, kind="ExternalOutput").ap()
    build(nc, **args, out=out)
    return _run(nc, [arrays], core_ids=[0]).results[0]["out"]
```

```python
import numpy as np
import concourse.bass as bass
from concourse import mybir
from contextlib import ExitStack

P = 128
DIM = 128
BATCHES = 8
SEQ = 512
TILES_B = SEQ // P
TILES = BATCHES * TILES_B
INNER = 1024
GROUPS = INNER // P
EXPERTS = 8
TOP_K = 2
HID0 = 256
UP0 = EXPERTS * HID0
HID1 = 512
CAP = int(1.25 * BATCHES * SEQ / EXPERTS)
SLOTS = EXPERTS * CAP
SLOT_TILES = CAP // P
SLOT_ROWS = SLOTS // P
HALF_CAP = CAP // 2
LN_EPS = 1e-5
OUT_EPS = 1e-6
TOPW_EPS = 1e-6
TOP_BIT = 29
OUTSIDE = P

PIPELINE0 = dict(
    project=(-0.11, 0.67), maxima=(0.97, 1.82), rows_of_maxima=(1.85, 1.85),
    probabilities=(2.21, 3.17), last_tile=(3.18, 3.24), mix=(3.51, 4.19),
    project_out=(4.24, 5.01),
    normalise=(-1.43, -0.56))
PIPELINE1 = dict(
    project=(0.12, 0.60), maxima=(1.02, 1.56), rows_of_maxima=(1.78, 1.78),
    probabilities=(2.21, 3.17), last_tile=(3.03, 3.30), mix=(3.53, 4.18),
    project_out=(4.15, 4.75), normalise=(-1.72, -0.89),
    collect=(-4.00, -2.00),
    route=(4.99, 6.20))
EXPERT_ROUNDS = 1.6
INTO_ATTENTION = 1.2
OUT_OF_ATTENTION = 2.7

C_IDENT = 0
C_BEFORE = C_IDENT + P
C_LOWER = C_BEFORE + P
C_SLOT0 = C_LOWER + EXPERTS * EXPERTS
C_SAME = C_SLOT0 + EXPERTS
C_COUNT = C_SAME + P
C_ROW = C_COUNT + P
C_WIDTH = C_ROW + 1


def constants():
    c = np.zeros((P, C_WIDTH), np.float32)
    c[:, C_IDENT:C_BEFORE] = np.eye(P)
    c[:, C_BEFORE:C_LOWER] = np.triu(np.ones((P, P)), 1)
    c[:, C_LOWER:C_SLOT0] = np.tril(np.ones((EXPERTS, EXPERTS)), -1).reshape(-1)
    c[:, C_SLOT0:C_SAME] = np.arange(EXPERTS) * CAP
    c[:, C_SAME:C_COUNT] = np.tile(np.eye(EXPERTS), (P // EXPERTS, P // EXPERTS))
    c[:, C_COUNT:C_ROW] = np.arange(P)
    c[:, C_ROW] = np.arange(P)
    return c


def merge(streams):
    live = [[start, i, (end - start) / steps, g] for i, (g, steps, (start, end)) in enumerate(streams)]
    while live:
        first = min(live)
        if next(first[3], "end") == "end":
            live.remove(first)
        else:
            first[0] += first[2]


def build(nc, x, w_qkv0, w_out0, b_out0, gamma0, beta0, gate0, up0, down0, bias0,
          w_qkv1, b_qk1, b_v1, w_out1, b_out1, router1, wg1, wu1, wd1, consts, out,
          batches=BATCHES, stages=range(1, 7)):
    fp32 = mybir.dt.float32
    f32r = mybir.dt.float32r
    i32 = mybir.dt.int32
    u32 = mybir.dt.uint32
    bf16 = mybir.dt.bfloat16
    ALU = mybir.AluOpType
    ACT = mybir.ActivationFunctionType
    AX = mybir.AxisListType

    ctx = ExitStack()
    with ctx:
        def sb(name, shape, dt=fp32):
            return ctx.enter_context(nc.sbuf_tensor(name, shape, dt))

        def sem(name):
            return ctx.enter_context(nc.semaphore(name))

        class Queue:

            def __init__(self, name):
                self.done = sem(f"{name}_done")
                self.count = 0
                self.steps = []

            def __call__(self, emit, *tickets, signal=True):
                if signal:
                    self.count += 1
                self.steps.append((emit, tickets, self.done if signal else None, 1))
                return (self.done, self.count) if signal else None

            def transfer(self, emit, arrival, *tickets):
                arrival.count += 16
                self.steps.append((emit, tickets, arrival.sem, 16))
                return (arrival.sem, arrival.count)

            def run(self, eng):
                waited = {}
                for emit, tickets, counter, by in self.steps:
                    for t in tickets:
                        if t is None:
                            continue
                        s, value = t
                        if waited.get(s.name, 0) < value:
                            eng.wait_ge(s, value)
                            waited[s.name] = value
                    ins = emit()
                    if counter is not None:
                        ins.then_inc(counter, by)

        class Arrival:

            def __init__(self, name):
                self.sem = sem(name)
                self.count = 0

            @property
            def all(self):
                return (self.sem, self.count)

        class Place:

            def __init__(self, ap, before):
                self.ap = ap
                self.before = before
                self.release(())

            def release(self, tickets):
                self.tickets = tickets
                self.in_use = False

            free = property(lambda self: (*self.tickets, *self.before), release)

        class Ring:
            def __init__(self, aps, before=()):
                self.places = [Place(a, before) for a in aps]

            def take(self):
                place = next(p for p in self.places if not p.in_use)
                self.places.remove(place)
                self.places.append(place)
                place.in_use = True
                return place

        pe, act, dve, pool, sp = (Queue(n) for n in ("pe", "act", "dve", "pool", "sp"))
        T_, S_, V_, G_, Y_ = nc.tensor, nc.scalar, nc.vector, nc.gpsimd, nc.sync

        X = sb("X", [P, TILES, DIM])
        cst = sb("cst", [P, C_WIDTH])
        ident = cst[:, C_IDENT:C_BEFORE]
        before = cst[:, C_BEFORE:C_LOWER]
        lower = cst[:, C_LOWER:C_SLOT0].rearrange("p (a e j) -> p a e j", a=1, e=EXPERTS)
        slot0 = cst[:, C_SLOT0:C_SAME].rearrange("p (a e) -> p a e", a=1)
        same_expert = cst[:, C_SAME:C_COUNT]
        count = cst[:, C_COUNT:C_ROW]
        row_number = cst[:, C_ROW:C_WIDTH]
        ones = sb("ones", [P, P])
        minus_half = sb("minus_half", [P, TILES_B])

        wqkv = sb("wqkv", [P, 3 * INNER])
        wout = sb("wout", [P, GROUPS, DIM])
        bqk = sb("bqk", [P, 2 * GROUPS])
        bv = sb("bv", [P, GROUPS])
        rows = sb("rows", [P, 4, DIM])
        gate_w = sb("gate_w", [P, EXPERTS])
        gate_b = sb("gate_b", [P, EXPERTS])
        router_w = sb("router_w", [P, EXPERTS])

        xn = Ring([sb(f"xn{i}", [P, TILES_B, DIM])[:, :, :] for i in range(2)])
        xT = Ring([sb(f"xT{i}", [P, SEQ])[:, :] for i in range(3)])
        moment_sets = Ring([(sb(f"stats{i}", [P, TILES_B, 6]), sb(f"mv{i}", [P, TILES_B, 2]),
                             sb(f"rstd{i}", [P, TILES_B])) for i in range(3)])

        ARENA = 80 * 256
        arena = sb("arena", [P, ARENA])

        class Carve:
            def __init__(self, at=0):
                self.at = at

            def __call__(self, *shape):
                n = int(np.prod(shape))
                ap = arena[:, self.at:self.at + n]
                self.at += n
                assert self.at <= ARENA, self.at
                if len(shape) == 1:
                    return ap
                names = " ".join("abcd"[:len(shape)])
                return ap.rearrange(f"p ({names}) -> p {names}", **dict(zip("abcd", shape)))

        psum = ctx.enter_context(nc.psum_tensor("psum", [P, 8, 512], fp32))
        bank = [psum[:, i, :] for i in range(8)]
        bank_s = Ring([bank[0], bank[1], bank[5]])
        bank_t = Ring(bank[2:4])
        bank_o = Ring(bank[4:5])
        banks_m = Ring(bank[6:8])

        tokens = nc.dram_tensor("tokens", (TILES * P, DIM), fp32, kind="Internal").ap()
        slots_out = nc.dram_tensor("slots_out", (SLOTS, DIM), fp32, kind="Internal").ap()

        got_up, got_down, got_qkv = (Arrival(f"got_{n}") for n in ("up", "down", "qkv"))
        got_small = Arrival("got_small")
        x_v = x.rearrange("b (t p) d -> b p t d", p=P)
        out_v = out.rearrange("b (t p) d -> b p t d", p=P)

        def load(dst, src, arrival, *tickets):
            return sp.transfer(lambda: Y_.dma_start(dst, src), arrival, *tickets)

        in_consts = load(cst[:, :], consts, Arrival("got_consts"))
        first_batch = load(X[:, 0:TILES_B, :], x_v[0], Arrival("got_x0"))
        for r, v in enumerate((b_out0, gamma0, beta0, b_out1)):
            load(rows[:, r, :], v.partition_broadcast(P), got_small)
        load(gate_b[:, :], bias0.partition_broadcast(P), got_small)
        load(gate_w[:, :], gate0, got_small)
        load(router_w[:, :], router1, got_small)
        load(bqk[:, :], b_qk1, got_small)
        load(bv[:, :], b_v1, got_small)
        small = got_small.all

        t_ones = dve(lambda: V_.memset(ones[:, :], 1.0))
        t_mh = dve(lambda: V_.memset(minus_half[:, :], -0.5))

        x_ready = [first_batch]
        for b in range(1, batches):
            x_ready.append(load(X[:, b * TILES_B:(b + 1) * TILES_B, :], x_v[b], Arrival(f"got_x{b}")))

        def moments(src_tiles, eps, *tickets):
            place = moment_sets.take()
            st, m, r = place.ap
            stats_of = [dve(lambda t=t: V_.bn_stats(st[:, t, :], src_tiles[t]), *tickets, *place.free)
                        for t in range(TILES_B)]
            for t in range(TILES_B):
                last = dve(lambda t=t: V_.bn_aggr(m[:, t, :], st[:, t, :]), stats_of[t], *place.free)
            var = dve(lambda: V_.tensor_scalar(r[:, :], m[:, :, 1], eps, None, ALU.add), last)
            place.ready = pool(lambda: G_.tensor_tensor(r[:, :], r[:, :], minus_half[:, :], ALU.pow),
                               var, t_mh)
            return place

        def standardise(dst, src_tiles, place, *tickets):
            st, m, r = place.ap
            for t in range(TILES_B):
                done = dve(lambda t=t: V_.tensor_scalar(dst[:, t, :], src_tiles[t], m[:, t, 0:1],
                                                        r[:, t:t + 1], ALU.subtract, ALU.mult),
                           place.ready, *tickets)
            place.free = (done,)
            return done

        def normalise(b, store=None):
            src = [X[:, b * TILES_B + t, :] for t in range(TILES_B)]
            m = moments(src, LN_EPS, x_ready[b])
            yield
            buf = xn.take()
            dst = buf.ap
            normed = standardise(dst, src, m, *buf.free)
            sent = store(buf, normed) if store else None
            yield
            bk = banks_m.take()
            for t in range(TILES_B):
                turned = pe(lambda t=t: T_.matmul(bk.ap[:, t * P:(t + 1) * P], dst[:, t, :], ident,
                                                  is_transpose=True),
                            normed, in_consts, *bk.free, signal=t == TILES_B - 1)
            buf.free = (turned, sent)
            place = xT.take()
            place.ready = act(lambda: S_.activation(place.ap, bk.ap, ACT.Copy), turned, *place.free)
            bk.free = (place.ready,)
            return place

        def drain(gen):
            for _ in gen:
                pass

        beats = sb("beats", [P, TILES_B, EXPERTS, EXPERTS])
        equal = sb("equal", [P, TILES_B, EXPERTS, EXPERTS])

        gate_last = [None]

        def ranks(value, rank, *tickets):
            vj = value.unsqueeze(2).to_broadcast([P, TILES_B, EXPERTS, EXPERTS])
            ve = value.unsqueeze(3).to_broadcast([P, TILES_B, EXPERTS, EXPERTS])
            low = lower.to_broadcast([P, TILES_B, EXPERTS, EXPERTS])
            a = dve(lambda: V_.tensor_tensor(beats[:, :, :, :], vj, ve, ALU.is_gt),
                    gate_last[0], *tickets)
            c = dve(lambda: V_.tensor_tensor(equal[:, :, :, :], vj, ve, ALU.is_equal), gate_last[0])
            c = dve(lambda: V_.tensor_tensor(equal[:, :, :, :], equal[:, :, :, :], low, ALU.mult),
                    c, in_consts)
            c = dve(lambda: V_.tensor_tensor(beats[:, :, :, :], beats[:, :, :, :],
                                             equal[:, :, :, :], ALU.add), a, c)
            c = dve(lambda: V_.tensor_reduce(rank, beats[:, :, :, :], AX.X, ALU.add), c)
            gate_last[0] = c
            return c

        gates = {n: [sb(f"{n}{i}", [P, TILES_B, EXPERTS]) for i in range(2)]
                 for n in ("score", "value", "rank", "weight")}
        gate_free = [(), ()]

        def logits(place, weights):
            bk = banks_m.take()
            for t in range(TILES_B):
                done = pe(lambda t=t: T_.matmul(bk.ap[:, t * EXPERTS:(t + 1) * EXPERTS],
                                                place.ap[:, t * P:(t + 1) * P], weights,
                                                start=True, stop=True),
                          place.ready, small, *bk.free, signal=t == TILES_B - 1)
            view = bk.ap[:, 0:TILES_B * EXPERTS].rearrange("p (t e) -> p t e", t=TILES_B)
            return bk, view, done

        QH, QL, KH, KL = range(4)
        halves = [sb(f"halves{i}", [P, 4, SEQ], f32r) for i in range(2)]
        halves_free = [(), ()]
        N_STACK = 3
        stack = [sb(f"stack{i}", [P, 2, 4, SEQ], f32r) for i in range(N_STACK)]
        stack_free = [()] * N_STACK
        stacked = [Arrival(f"stacked{i}") for i in range(N_STACK)]
        max_rows = [Arrival(f"max_rows{i}") for i in range(N_STACK)]
        N_VALUES = 4
        values = [sb(f"values{i}", [P, TILES_B, P]) for i in range(N_VALUES)]
        values_free = [()] * N_VALUES
        N_PROB = 5
        top = [sb(f"top{i}", [P, 16]) for i in range(2)]
        top_free = [(), ()]
        mh = [sb(f"mh{i}", [16, P], f32r) for i in range(2)]
        ml = [sb(f"ml{i}", [16, P], f32r) for i in range(2)]
        m_free = [(), ()]

        wqkv_free = [()]
        wout_free = [()]

        def split(hi, lo, value, *tickets):
            h_ = act(lambda: S_.activation(hi, value, ACT.Copy), *tickets)
            l_ = dve(lambda: V_.tensor_tensor(lo, value, hi.bitcast(fp32), ALU.subtract), h_, *tickets)
            return h_, l_

        def three_products(bk, out_ap, weights, moving, *tickets):
            for i, (w, m) in enumerate(((0, 0), (0, 1), (1, 0))):
                done = pe(lambda i=i, w=w, m=m: T_.matmul(out_ap, weights[w], moving[m],
                                                          start=i == 0, stop=i == 2),
                          *tickets, *bk.free, signal=i == 2)
            return done

        def experts0(streams, at, weights, weights_free, hid_at, hid_free, stacks, after=None):
            up = weights[0]
            up_halves = stack[stacks[0]].rearrange("p s h q -> p s (h q)")
            x_halves = stack[stacks[1]]
            up_split, x_free = [], [(), ()]
            down = [w.rearrange("p (e c d) -> p e c d", e=EXPERTS // 2, c=2) for w in weights[1:]]
            hid, handed, w_up, w_down = [], [], [], []

            gate = {}

            def prepare(b):
                place = yield from normalise(b)
                g = b % 2
                score, value, rank, weight = (gates[n][g] for n in ("score", "value", "rank", "weight"))
                bk, view, done = logits(place, gate_w[:, :])
                halves_x = x_halves[:, g, 0:2, :]
                x_split = split(halves_x[:, 0, :], halves_x[:, 1, :], place.ap, place.ready,
                                *(x_free[g] or stack_free[stacks[1]]))
                place.free = (done, *x_split)
                s = act(lambda: S_.activation(score[:, :, :], view, ACT.Sigmoid), done, *gate_free[g])
                bk.free = (s,)
                bias = gate_b[:, :].unsqueeze(1).to_broadcast([P, TILES_B, EXPERTS])
                v = dve(lambda: V_.tensor_tensor(value[:, :, :], score[:, :, :], bias, ALU.add),
                        s, small, *gate_free[g])
                yield
                r = ranks(value[:, :, :], rank[:, :, :], v)
                yield
                v = dve(lambda: V_.scalar_tensor_tensor(out=value[:, :, :], in0=rank[:, :, :],
                                                        scalar=float(TOP_K), in1=score[:, :, :],
                                                        op0=ALU.is_lt, op1=ALU.mult), r)
                w = dve(lambda: V_.scalar_tensor_tensor(out=weight[:, :, :], in0=value[:, :, :],
                                                        scalar=0.5, in1=value[:, :, :],
                                                        op0=ALU.mult, op1=ALU.mult), v)
                gate[b] = (halves_x, x_split, weight, w)
                yield

            def compute(b):
                halves_x, x_split, weight, w = gate[b]
                steps = []
                if b == 0:
                    carve = Carve(hid_at)
                    hid.append(Ring([carve(2, SEQ) for _ in range(3)], hid_free()))

                def up_step(e):
                    h = hid[0].take()
                    squares = []
                    for c in range(2):
                        bk = bank_s.take()
                        col = (e * 2 + c) * P
                        u = three_products(bk, bk.ap, (up_halves[:, 0, col:col + P], up_halves[:, 1, col:col + P]),
                                           (halves_x[:, 0, :], halves_x[:, 1, :]),
                                           *up_split[col // SEQ], *x_split)
                        part = h.ap[:, c, :]
                        if c:
                            r = dve(lambda bk=bk, part=part: V_.tensor_scalar(part, bk.ap, 0.0, None, ALU.max),
                                    u, *h.free)
                        else:
                            r = act(lambda bk=bk, part=part: S_.activation(part, bk.ap, ACT.Relu), u, *h.free)
                        squares.append(act(lambda part=part: S_.activation(part, part, ACT.Square), r))
                        bk.free = (r,)
                    if e == EXPERTS - 1:
                        x_free[b % 2] = (u,)
                        if b == batches - 1:
                            stack_free[stacks[0]] = stack_free[stacks[1]] = (u,)
                    steps.append((h, squares))

                def down_step(e):
                    h, squares = steps[e]
                    bk = bank_t.take()
                    for t in range(TILES_B):
                        for c in range(2):
                            d = pe(lambda t=t, c=c: T_.matmul(bk.ap[:, t * P:(t + 1) * P],
                                                              h.ap[:, c, t * P:(t + 1) * P],
                                                              down[2 * e // EXPERTS][:, e % (EXPERTS // 2), c, :],
                                                              start=c == 0, stop=c == 1),
                                   *squares, w_down[0], *bk.free, signal=t == TILES_B - 1 and c == 1)
                    h.free = (d,)
                    for t in range(TILES_B):
                        tile = b * TILES_B + t
                        a = dve(lambda t=t, tile=tile: V_.scalar_tensor_tensor(
                            out=X[:, tile, :], in0=bk.ap[:, t * P:(t + 1) * P],
                            scalar=weight[:, t, e:e + 1], in1=X[:, tile, :],
                            op0=ALU.mult, op1=ALU.add), d, w, x_ready[b])
                    bk.free = (a,)
                    x_ready[b] = a
                    return a

                up_step(0)
                yield
                for e in range(EXPERTS):
                    if e + 1 < EXPERTS:
                        up_step(e + 1)
                        yield
                    last = down_step(e)
                    yield
                gate_free[b % 2] = (last,)
                if b == batches - 1:
                    handed.extend([(pe.done, pe.count), (dve.done, dve.count), (act.done, act.count)])
                    wqkv_free[0] = tuple(handed)

            def load_weights():
                w_up.append(load(up, up0, got_up, *weights_free()))
                source = down0.rearrange("p (h e c) d -> h p e c d", h=2, c=2)
                for h in range(2):
                    load(down[h], source[h], got_down, *weights_free())
                w_down.append(got_down.all)
                yield
                for c in range(0, UP0, SEQ):
                    cols = slice(c, c + SEQ)
                    up_split.append(split(up_halves[:, 0, cols], up_halves[:, 1, cols], up[:, cols],
                                          w_up[0], *stack_free[stacks[0]]))
                yield

            streams.append((load_weights(), 2, (at - 1, at + 0.9)))
            for b in range(batches):
                here = at + b * EXPERT_ROUNDS
                streams.append((compute(b), 16, (here, here + EXPERT_ROUNDS)))
                streams.append((prepare(b), 5, (here - EXPERT_ROUNDS, here - 0.05)))
                if after:
                    streams.append((after(b), 3, (here + EXPERT_ROUNDS, here + 2 * EXPERT_ROUNDS)))
            return handed

        recips = Ring([sb(f"recips{i}", [P, TILES_B, 4])[:, :, :] for i in range(2)])

        def attention(wqkv_src, wout_src, heads, width, bias_qk, finish, pipeline, streams, at,
                      before, first=None, after=None):
            scale = float(width) ** -0.5
            turned = heads == 4
            if heads == 4:
                copies = ((0, 0, QH, KH), (32, 0, QL, KH), (64, 0, QH, KL))
                parts = ((96, 98, 0),)
            else:
                copies = ((0, 0, QH, KH), (64, 0, QL, KH), (0, 2, QH, KL))
                parts = ((P, P, 0), (64, 66, 2))
            max_at, max_slot = parts[-1][0], parts[-1][2]
            carve = Carve()
            prob = Ring([carve(heads, SEQ) for _ in range(N_PROB)], before)
            sums = Ring([carve(heads, SEQ) for _ in range(2)], before)
            inv = Ring([carve(SEQ) for _ in range(2)], before)
            weighted = Ring([carve(SEQ) for _ in range(2)], before)
            mixed = carve(GROUPS, SEQ)
            tiles_prob = list(prob.places)
            mixed_free = [before]
            t_w = []

            def load_weights():
                load(wqkv[:, :], wqkv_src, got_qkv, *wqkv_free[0])
                load(wout[:, :, :], wout_src, got_qkv, *wout_free[0])
                t_w.append(got_qkv.all)
                yield

            streams.append((load_weights(), 1, (at - GROUPS, at - GROUPS)))
            t_ones_rows = {}
            places, info = {}, {}

            def project(b, g, n):
                hv, st, i, s = halves[n % 2], stack[n % N_STACK], n % 2, n % N_STACK
                place = places[b]
                hf = halves_free[i]
                split = []
                for which, hi, lo in ((0, QH, QL), (1, KH, KL)):
                    bk = banks_m.take()
                    col = which * INNER + g * P
                    p_ = pe(lambda bk=bk, col=col: T_.matmul(bk.ap, wqkv[:, col:col + P], place.ap,
                                                             start=True, stop=True),
                            *t_w, place.ready, *bk.free)
                    if bias_qk:
                        bias = bqk[:, which * GROUPS + g:which * GROUPS + g + 1]
                        h_ = act(lambda bk=bk, hi=hi, bias=bias: S_.activation(
                            hv[:, hi, :], bk.ap, ACT.Identity, bias=bias), p_, small, *hf)
                        l_ = dve(lambda bk=bk, hi=hi, lo=lo, bias=bias: V_.scalar_tensor_tensor(
                            out=hv[:, lo, :], in0=bk.ap, scalar=bias, in1=hv[:, hi, :].bitcast(fp32),
                            op0=ALU.add, op1=ALU.subtract), h_, *hf)
                    else:
                        h_ = act(lambda bk=bk, hi=hi: S_.activation(hv[:, hi, :], bk.ap, ACT.Copy), p_, *hf)
                        l_ = dve(lambda bk=bk, hi=hi, lo=lo: V_.tensor_tensor(
                            hv[:, lo, :], bk.ap, hv[:, hi, :].bitcast(fp32), ALU.subtract), h_, *hf)
                    bk.free = (l_,)
                    split += [h_, l_]
                    yield
                if n < N_STACK:
                    t_ones_rows[s] = dve(lambda: V_.memset(
                        st[max_at:max_at + 2, 1, max_slot:max_slot + heads, :].bitcast(fp32), 1.0),
                        *stack_free[s])
                for at, slot, q_part, k_part in copies:
                    for h in range(heads):
                        sp.transfer(lambda at=at, slot=slot, q_part=q_part, k_part=k_part, h=h: Y_.dma_start(
                            st[at:at + width, :, slot + h, :].bitcast(fp32),
                            hv[width * h:width * (h + 1), q_part:k_part + 1:k_part - q_part, :].bitcast(fp32)),
                            stacked[s], *split, *stack_free[s])
                halves_free[i] = (stacked[s].all,)
                bk = banks_m.take()
                for t in range(TILES_B):
                    p_ = pe(lambda t=t, bk=bk: T_.matmul(bk.ap[:, t * P:(t + 1) * P],
                                                         place.ap[:, t * P:(t + 1) * P],
                                                         wqkv[:, 2 * INNER + g * P:2 * INNER + (g + 1) * P],
                                                         start=True, stop=True),
                            *t_w, place.ready, *bk.free, signal=t == TILES_B - 1)
                if g == GROUPS - 1:
                    place.free = (p_,)
                    wqkv_free[0] = (p_,)
                v_ = act(lambda bk=bk: S_.activation(values[n % N_VALUES][:, :, :], bk.ap.rearrange(
                    "p (t f) -> p t f", t=TILES_B), ACT.Copy), p_, *values_free[n % N_VALUES])
                bk.free = (v_,)
                info[n] = dict(stacked=stacked[s].all, values=v_)
                yield

            def product(bk, st, side, h, cols, with_max, *tickets):
                for r, (plain, full, slot) in enumerate(parts):
                    k = full if with_max else plain
                    last = r == len(parts) - 1
                    done = pe(lambda k=k, slot=slot, r=r, last=last: T_.matmul(
                        bk.ap, st[0:k, side, slot + h, cols], st[0:k, 1 - side, slot + h, :],
                        start=r == 0, stop=last), *tickets, *bk.free, signal=last)
                return done

            def maxima(b, g, n):
                st, i = stack[n % N_STACK], n % 2
                d = info[n]
                for h in range(heads):
                    for qt in range(TILES_B):
                        bk = bank_s.take()
                        s_ = product(bk, st, 0, h, slice(qt * P, (qt + 1) * P), False, d["stacked"])
                        m_ = dve(lambda bk=bk, h=h, qt=qt: V_.reduce_max(
                            top[i][:, h * TILES_B + qt:h * TILES_B + qt + 1], bk.ap, AX.X),
                            s_, *top_free[i])
                        bk.free = (m_,)
                        yield
                d["top"] = m_

            def rows_of_maxima(n):
                st, i, s = stack[n % N_STACK], n % 2, n % N_STACK
                d = info[n]
                n_top = heads * TILES_B
                bk = banks_m.take()
                t_ = pe(lambda bk=bk: T_.matmul(bk.ap[0:n_top, 0:P], top[i][:, 0:n_top], ident,
                                                is_transpose=True), d["top"], *bk.free)
                top_free[i] = (t_,)
                a_ = act(lambda bk=bk: S_.activation(mh[i][0:n_top, :], bk.ap[0:n_top, 0:P], ACT.Copy,
                                                     scale=-1.0), t_, *m_free[i])
                b_ = dve(lambda bk=bk: V_.scalar_tensor_tensor(
                    out=ml[i][0:n_top, :], in0=bk.ap[0:n_top, 0:P], scalar=-1.0,
                    in1=mh[i][0:n_top, :].bitcast(fp32), op0=ALU.mult, op1=ALU.subtract),
                    a_, *m_free[i])
                bk.free = (b_,)
                for r, part in enumerate((mh[i], ml[i])):
                    sp.transfer(lambda r=r, part=part: Y_.dma_start(
                        st[max_at + r:max_at + r + 1, 0, max_slot:max_slot + heads, :].rearrange(
                            "a h (t q) -> a (h t) q", t=TILES_B).bitcast(fp32),
                        part[0:n_top, :].bitcast(fp32)), max_rows[s], a_, b_)
                m_free[i] = (max_rows[s].all,)
                d["max_rows"] = max_rows[s].all
                yield

            def weigh(n, kt):
                d = info[n]
                pr, e_ = d["prob"][kt]
                if kt == 0:
                    d["o"] = bank_o.take()
                for h in range(heads):
                    c = slice(width * h, width * (h + 1))
                    v_ = pe(lambda c=c, h=h: T_.matmul(
                        d["o"].ap[c, :], values[n % N_VALUES][:, kt, c], pr.ap[:, h, :],
                        start=kt == 0, stop=kt == TILES_B - 1, tile_position=(0, width * h)),
                        e_, d["values"], *d["o"].free, signal=h == heads - 1)
                d["weighed"] = v_
                pr.free = (v_, d["summed"][kt])

            def probabilities(b, g, n):
                st, s = stack[n % N_STACK], n % N_STACK
                d = info[n]
                d["prob"], d["summed"] = [], []
                total = d["total"] = sums.take()
                for kt in range(TILES_B):
                    pr = prob.take()
                    for h in range(heads):
                        bk = bank_t.take()
                        s_ = product(bk, st, 1, h, slice(kt * P, (kt + 1) * P), True,
                                     d["stacked"], d["max_rows"], t_ones_rows[s])
                        e_ = act(lambda bk=bk, pr=pr, h=h: S_.activation(pr.ap[:, h, :], bk.ap, ACT.Exp,
                                                                         scale=scale), s_, *pr.free)
                        bk.free = (e_,)
                        yield
                    d["prob"].append((pr, e_))
                    if kt:
                        before_ = d["prob"][0][0].ap if kt == 1 else total.ap
                        for part in (slice(i, i + 2) for i in range(0, heads, 2)):
                            a_ = pool(lambda old=before_, pr=pr, part=part: G_.tensor_tensor(
                                total.ap[:, part, :], old[:, part, :], pr.ap[:, part, :], ALU.add),
                                e_, *total.free, *d["summed"][-1:])
                        d["summed"] += [a_] if kt > 1 else [a_, a_]
                    if kt:
                        weigh(n, kt - 1)
                        yield
                stack_free[s] = (s_,)

            def last_tile(n):
                weigh(n, TILES_B - 1)
                d = info[n]
                values_free[n % N_VALUES] = (d["weighed"],)
                yield
                d["weighted"] = weighted.take()
                d["copied"] = act(lambda: S_.activation(d["weighted"].ap, d["o"].ap, ACT.Copy),
                                  d["weighed"], *d["weighted"].free)
                d["o"].free = (d["copied"],)
                yield

            def mix(b, g, n):
                d = info.pop(n)
                dn = banks_m.take()
                total = d["total"]
                for h in range(heads):
                    c = slice(width * h, width * (h + 1))
                    n_ = pe(lambda c=c, h=h: T_.matmul(
                        dn.ap[c, :], ones[:, 0:width], total.ap[:, h, :],
                        start=True, stop=True, tile_position=(0, width * h)),
                        d["summed"][-1], t_ones, *dn.free, signal=h == heads - 1)
                total.free = (n_,)
                yield
                r = inv.take()
                if turned:
                    c_ = act(lambda: S_.activation(r.ap, dn.ap, ACT.Copy), n_, *r.free)
                    dn.free = (c_,)
                    yield
                    bk = banks_m.take()
                    t_ = turn(bk, r.ap, c_)
                    yield
                    small_r = recips.take()
                    r_ = dve(lambda: V_.reciprocal(small_r.ap, bk.ap.rearrange(
                        "p (t h w) -> p t h w", t=TILES_B, h=heads)[:, :, :, 0]), t_, *small_r.free)
                    bk.free = (r_,)
                    c_ = act(lambda: S_.activation(
                        r.ap.rearrange("p (t h w) -> p t h w", t=TILES_B, h=heads),
                        small_r.ap.unsqueeze(3).to_broadcast([P, TILES_B, heads, width]), ACT.Copy), r_)
                    small_r.free = (c_,)
                    yield
                    inverse = banks_m.take()
                    r_ = turn(inverse, r.ap, c_)
                    r.free = (r_,)
                    yield
                else:
                    for q in range(TILES_B):
                        c = slice(q * P, (q + 1) * P)
                        r_ = dve(lambda c=c: V_.reciprocal(r.ap[:, c], dn.ap[:, c]), n_, *r.free)
                        yield
                    dn.free = (r_,)
                    inverse = r
                w = d["weighted"]
                o_ = dve(lambda: V_.tensor_tensor(mixed[:, g, :], w.ap, inverse.ap, ALU.mult),
                         d["copied"], r_, *mixed_free[0])
                w.free = (o_,)
                inverse.free = (o_,)
                if bias_qk:
                    o_ = dve(lambda: V_.tensor_scalar(mixed[:, g, :], mixed[:, g, :], bv[:, g:g + 1],
                                                      None, ALU.add), o_, small)
                d_mixed[0] = o_
                yield

            d_mixed = [None]

            def turn(bk, ap, ticket):
                for t in range(TILES_B):
                    c = slice(t * P, (t + 1) * P)
                    done = pe(lambda c=c: T_.matmul(bk.ap[:, c], ap[:, c], ident, is_transpose=True),
                              ticket, *bk.free, signal=t == TILES_B - 1)
                return done

            def project_out(b):
                bk = banks_m.take()
                for t in range(TILES_B):
                    for gg in range(GROUPS):
                        p_ = pe(lambda t=t, gg=gg: T_.matmul(bk.ap[:, t * P:(t + 1) * P],
                                                             mixed[:, gg, t * P:(t + 1) * P],
                                                             wout[:, gg, :],
                                                             start=gg == 0, stop=gg == GROUPS - 1),
                                d_mixed[0], *t_w, *bk.free,
                                signal=t == TILES_B - 1 and gg == GROUPS - 1)
                        if gg % 4 == 3:
                            yield
                mixed_free[0] = wout_free[0] = (p_,)
                yield from finish(b, bk, p_)
                if b == batches - 1:
                    handed.extend([(pe.done, pe.count), (dve.done, dve.count), (act.done, act.count),
                                   (pool.done, pool.count)])

            order = [(b, g) for b in range(batches) for g in range(GROUPS)]
            handed = []

            def queue(gen, steps, n, stage):
                when = pipeline[stage]
                streams.append((gen, steps, (at + n + when[0], at + n + when[1])))

            def ahead(b):
                places[b] = yield from normalise(b)
                yield

            for n, (b, g) in enumerate(order):
                queue(last_tile(n), 2, n, "last_tile")
                queue(project(b, g, n), 3, n, "project")
                queue(maxima(b, g, n), heads * TILES_B, n, "maxima")
                queue(rows_of_maxima(n), 1, n, "rows_of_maxima")
                queue(probabilities(b, g, n), (heads + 1) * TILES_B, n, "probabilities")
                queue(mix(b, g, n), 6, n, "mix")
                if g == GROUPS - 1:
                    queue(project_out(b), 12, n, "project_out")
                if g == 0:
                    queue(ahead(b), 3, n, "normalise")
                    if first:
                        queue(first(b), TILES_B * TOP_K, n, "collect")
                if g == GROUPS - 1 and after:
                    queue(after(b), 4, n, "route")
            return handed, lambda i: [t for p in tiles_prob[i:i + 2] for t in p.free]

        y = [sb("y", [P, TILES_B, DIM])]
        y_free = [()]

        def row(r):
            return rows[:, r, :].unsqueeze(1).to_broadcast([P, TILES_B, DIM])

        def finish0(b, bk, p_):
            i = 0
            view = bk.ap.rearrange("p (t d) -> p t d", t=TILES_B)
            a = dve(lambda: V_.tensor_tensor(y[i][:, :, :], view, row(0), ALU.add), p_, small, *y_free[i])
            bk.free = (a,)
            yield
            src = [y[i][:, t, :] for t in range(TILES_B)]
            m = moments(src, OUT_EPS, a)
            yield
            a = standardise(y[i][:, :, :], src, m)
            yield
            a = dve(lambda: V_.tensor_tensor(y[i][:, :, :], y[i][:, :, :], row(1), ALU.mult), a)
            a = dve(lambda: V_.tensor_tensor(y[i][:, :, :], y[i][:, :, :], row(2), ALU.add), a)
            xb = X[:, b * TILES_B:(b + 1) * TILES_B, :]
            a = dve(lambda: V_.tensor_tensor(xb, xb, y[i][:, :, :], ALU.add), a, x_ready[b])
            y_free[i] = (a,)
            x_ready[b] = a
            yield

        def finish1(b, bk, p_):
            i = 0
            view = bk.ap.rearrange("p (t d) -> p t d", t=TILES_B)
            a = dve(lambda: V_.tensor_tensor(y[i][:, :, :], view, row(3), ALU.add), p_, small, *y_free[i])
            bk.free = (a,)
            xb = X[:, b * TILES_B:(b + 1) * TILES_B, :]
            a = dve(lambda: V_.tensor_tensor(xb, xb, y[i][:, :, :], ALU.add), a, x_ready[b])
            y_free[i] = (a,)
            x_ready[b] = a
            yield

        N_GOT = 8
        tiles = batches * TILES_B
        keep_at = ARENA - (2 * TILES * EXPERTS + 2 * TOP_K * TILES + N_GOT * DIM)
        keep = Carve(keep_at)
        W = keep(tiles, EXPERTS)
        R = keep(tiles, EXPERTS)
        idx_in = keep(TOP_K, tiles)
        w_k = keep(TOP_K, tiles)
        got = Ring([keep(DIM) for _ in range(N_GOT)])
        gathered = {id(p): Arrival(f"gathered{i}") for i, p in enumerate(got.places)}
        r_score, r_value = (sb(n, [P, TILES_B, EXPERTS]) for n in ("r_score", "r_value"))
        soft = [sb(f"soft{i}", [P, TILES_B])[:, :] for i in range(4)]
        tokens_v = tokens.rearrange("(t p) d -> p t d", p=P)
        tokens_stored = {id(p): Arrival(f"tokens_stored{i}") for i, p in enumerate(xn.places)}
        rows_ready = [Arrival(f"rows_ready{i}") for i in range(2)]
        slots_stored = [Arrival(f"slots_stored{i}") for i in range(2)]
        gate_up_in = [Arrival(f"gate_up_in{i}") for i in range(2)]
        down_in = [Arrival(f"down_in{i}") for i in range(2)]
        dram_free = [()]
        routed = [None]

        def route(b):
            here = slice(b * TILES_B, (b + 1) * TILES_B)

            def store(buf, normed):
                return sp.transfer(lambda: Y_.dma_start(tokens_v[:, here, :], buf.ap),
                                   tokens_stored[id(buf)], normed, *rows_gathered[0])

            place = yield from normalise(b, store)
            bk, view, done = logits(place, router_w[:, :])
            place.free = (done,)
            wide = [P, TILES_B, EXPERTS]
            top_, sum_, sel_, inv_ = soft
            f = routed[0]
            a = dve(lambda: V_.tensor_reduce(top_, view, AX.X, ALU.max), done, f)
            a = dve(lambda: V_.tensor_tensor(r_value[:, :, :], view, top_.unsqueeze(2).to_broadcast(wide),
                                             ALU.subtract), a)
            bk.free = (a,)
            e_ = act(lambda: S_.activation(r_score[:, :, :], r_value[:, :, :], ACT.Exp), a)
            yield
            a = dve(lambda: V_.tensor_reduce(sum_, r_score[:, :, :], AX.X, ALU.add), e_)
            a = dve(lambda: V_.reciprocal(inv_, sum_), a)
            a = dve(lambda: V_.tensor_tensor(r_score[:, :, :], r_score[:, :, :],
                                             inv_.unsqueeze(2).to_broadcast(wide), ALU.mult), a)
            a = ranks(r_score[:, :, :], R[:, here, :], a, *keep_free[0])
            a = dve(lambda: V_.scalar_tensor_tensor(out=r_value[:, :, :], in0=R[:, here, :],
                                                    scalar=float(TOP_K), in1=r_score[:, :, :],
                                                    op0=ALU.is_lt, op1=ALU.mult), a)
            a = dve(lambda: V_.tensor_reduce(sel_, r_value[:, :, :], AX.X, ALU.add), a)
            a = dve(lambda: V_.tensor_scalar(sel_, sel_, TOPW_EPS, None, ALU.add), a)
            a = dve(lambda: V_.reciprocal(inv_, sel_), a)
            a = dve(lambda: V_.tensor_tensor(W[:, here, :], r_value[:, :, :],
                                             inv_.unsqueeze(2).to_broadcast(wide), ALU.mult), a)
            routed[0] = a
            yield

        def collect(b):
            for t in range(b * TILES_B, (b + 1) * TILES_B):
                for k in range(TOP_K):
                    place = got.take()
                    g_ = pool.transfer(lambda t=t, k=k, place=place: G_.indirect_dma_start(
                        place.ap, None, slots_out,
                        bass.IndirectOffsetOnAxis(ap=idx_in[:, k, t:t + 1].bitcast(u32), axis=0),
                        bounds_check=SLOTS - 1, oob_is_err=False),
                        gathered[id(place)], *outputs_stored[0], *place.free)
                    a = dve(lambda t=t, k=k, place=place: V_.scalar_tensor_tensor(
                        out=X[:, t, :], in0=place.ap, scalar=w_k[:, k, t:t + 1], in1=X[:, t, :],
                        op0=ALU.mult, op1=ALU.add), g_, x_ready[b])
                    place.free = (a,)
                    x_ready[b] = a
                    yield
            dram_free[0] = (a,)

        keep_free = [()]
        rows_gathered = [()]
        outputs_stored = [()]

        def experts1(region_free):
            carve = Carve()
            wg, wu, wd = (wqkv[:, i * 2 * HID1:(i + 1) * 2 * HID1].rearrange("p (e f) -> p e f", e=2)
                          for i in range(3))
            wd = wd.rearrange("p e (f d) -> p e f d", d=DIM)
            ge = carve(tiles, EXPERTS)
            flags = carve(2, tiles, EXPERTS)
            scan = [carve(2, tiles, EXPERTS) for _ in range(2)]
            tmp = [carve(tiles, EXPERTS) for _ in range(3)]
            weightT = carve(tiles * EXPERTS)
            reach = carve(tiles * EXPERTS)
            thr, cand, step = (carve(1) for _ in range(3))
            cnt = carve(1).bitcast(bf16)[:, 0:1]
            same_bf16 = carve(P // 2).bitcast(bf16)
            thr_wide = carve(P)
            slot_k = carve(2, tiles)
            kept_k = carve(2, tiles)
            within = carve(2, tiles)
            slot_row = carve(2, tiles)
            row_hot = carve(2 * tiles, 2 * SLOT_ROWS // 2).bitcast(bf16).rearrange(
                "p j (x r) -> p j x r", x=2)
            within_hot = Ring([carve(16, P // 2).bitcast(bf16) for _ in range(2)])
            token_of = carve(SLOT_ROWS)
            rows_in = [carve(SLOT_TILES, DIM) for _ in range(2)]
            rows_free = [(), ()]
            sig = Ring([carve(HALF_CAP) for _ in range(3)])
            hid = Ring([carve(HID1 // P, CAP) for _ in range(2)])
            eo = Ring([carve(SLOT_TILES, DIM) for _ in range(2)])
            assert carve.at <= keep_at

            t_gate_up, t_down = {}, {}

            def load_gate_up(e, *free):
                i = e % 2
                load(wg[:, i, :], wg1[:, e, :], gate_up_in[i], *free)
                load(wu[:, i, :], wu1[:, e, :], gate_up_in[i], *free)
                t_gate_up[e] = gate_up_in[i].all

            def load_down(e, *free):
                t_down[e] = load(wd[:, e % 2, :, :], wd1[:, e, :, :], down_in[e % 2], *free)

            for e in range(2):
                load_gate_up(e, *wqkv_free[0])
                load_down(e, *wqkv_free[0])
            a = routed[0]

            def bits(v):
                return v.bitcast(i32)

            bk = banks_m.take()
            tiles_row = P // EXPERTS
            for i in range(tiles // tiles_row):
                t_ = pe(lambda bk=bk, i=i: T_.matmul(bk.ap[:, i * P:(i + 1) * P],
                                              W[:, i * tiles_row:(i + 1) * tiles_row, :].rearrange("p t e -> p (t e)"),
                                              ident, is_transpose=True), a, *bk.free)
            c = dve(lambda bk=bk: V_.tensor_copy(weightT, bk.ap[:, 0:tiles * EXPERTS]), t_, *region_free)
            bk.free = (c,)
            t0 = dve(lambda: V_.tensor_copy(same_bf16, same_expert), in_consts)
            t0 = dve(lambda: V_.memset(bits(thr), 0), t0)
            a = dve(lambda: V_.memset(bits(cand), 1 << TOP_BIT))
            for bit in range(TOP_BIT, -1, -1):
                a = dve(lambda: V_.tensor_scalar(reach, weightT, cand, None, ALU.is_ge, ALU.add,
                                                 accum_out=cnt), a, c)
                bk = banks_m.take()
                c_ = pe(lambda bk=bk: T_.matmul(bk.ap[:, 0:1], same_bf16, cnt,
                                                start=True, stop=True), a, t0, *bk.free)
                a = dve(lambda bk=bk, bit=bit: V_.tensor_scalar(bits(step), bk.ap[:, 0:1],
                                                                float(CAP), float(1 << bit),
                                                                ALU.is_ge, ALU.mult), c_)
                bk.free = (a,)
                if bit:
                    n_ = dve(lambda bit=bit: V_.scalar_tensor_tensor(
                        out=bits(cand), in0=bits(step), scalar=1 << (bit - 1), in1=bits(thr),
                        op0=ALU.bitwise_or, op1=ALU.bitwise_or), a, t0)
                t0 = dve(lambda: V_.tensor_tensor(bits(thr), bits(thr), bits(step), ALU.bitwise_or), a)
                a = n_
            a = dve(lambda: V_.tensor_copy(thr_wide, thr.to_broadcast([P, P])), t0)
            bk = banks_m.take()
            t_ = pe(lambda bk=bk: T_.matmul(bk.ap[:, 0:P], thr_wide, ident, is_transpose=True), a, *bk.free)
            thr_row = bk.ap[:, 0:EXPERTS]
            wide = [P, tiles, EXPERTS]
            a = t_

            thr_b = thr_row.unsqueeze(1).to_broadcast(wide)
            over, tied = flags[:, 0], flags[:, 1]
            a0 = dve(lambda: V_.tensor_tensor(over, W, thr_b, ALU.is_gt), a)
            a = dve(lambda: V_.tensor_tensor(tied, W, thr_b, ALU.is_equal), a)
            bk.free = (a,)
            a = dve(lambda: V_.scalar_tensor_tensor(out=tied, in0=W, scalar=0.0, in1=tied,
                                                    op0=ALU.is_gt, op1=ALU.mult), a)
            flat = "p a t e -> p (a t e)"
            inside, totals = bank_t.take(), bank_t.take()
            n_flags = 2 * tiles * EXPERTS
            i_ = pe(lambda: T_.matmul(inside.ap[:, 0:n_flags], before, flags.rearrange(flat),
                                      start=True, stop=True), a0, a, in_consts, *inside.free)
            t_ = pe(lambda: T_.matmul(totals.ap[:, 0:n_flags], ones[:, :], flags.rearrange(flat),
                                      start=True, stop=True), *totals.free)
            a = dve(lambda: V_.tensor_copy(scan[0].rearrange(flat), totals.ap[:, 0:n_flags]), t_)
            totals.free = (a,)
            s, shift = 0, 1
            while shift < tiles:
                src, dst = scan[s], scan[1 - s]
                b1 = dve(lambda src=src, dst=dst, k=shift: V_.tensor_tensor(
                    dst[:, :, k:, :], src[:, :, k:, :], src[:, :, :tiles - k, :], ALU.add), a)
                a = dve(lambda src=src, dst=dst, k=shift: V_.tensor_copy(
                    dst[:, :, :k, :], src[:, :, :k, :]), b1)
                s, shift = 1 - s, shift * 2
            upto, pos = scan[s], scan[1 - s]
            a = dve(lambda: V_.tensor_copy(pos.rearrange(flat), inside.ap[:, 0:n_flags]), a, i_)
            inside.free = (a,)
            if tiles > 1:
                a = dve(lambda: V_.tensor_tensor(pos[:, :, 1:, :], pos[:, :, 1:, :],
                                                 upto[:, :, :tiles - 1, :], ALU.add), a)
            all_over = upto[:, 0, tiles - 1:tiles, :].to_broadcast(wide)
            pos_o, pos_t = pos[:, 0], pos[:, 1]
            a = dve(lambda: V_.tensor_tensor(pos_t, pos_t, all_over, ALU.add), a)
            a = dve(lambda: V_.scalar_tensor_tensor(out=tied, in0=pos_t, scalar=float(CAP), in1=tied,
                                                    op0=ALU.is_lt, op1=ALU.mult), a)
            m0, m1, m2 = tmp
            kept = ge
            a = dve(lambda: V_.tensor_tensor(m0, over, pos_o, ALU.mult), a)
            a = dve(lambda: V_.tensor_tensor(m1, tied, pos_t, ALU.mult), a)
            a = dve(lambda: V_.tensor_tensor(m0, m0, m1, ALU.add), a)
            a = dve(lambda: V_.tensor_tensor(m0, m0, slot0.to_broadcast(wide), ALU.add), a)
            a = dve(lambda: V_.tensor_tensor(kept, over, tied, ALU.add), a)
            for k in range(TOP_K):
                a = dve(lambda k=k: V_.scalar_tensor_tensor(out=m1, in0=R, scalar=float(k), in1=kept,
                                                            op0=ALU.is_equal, op1=ALU.mult), a)
                a = dve(lambda k=k: V_.tensor_reduce(kept_k[:, k, :], m1, AX.X, ALU.add), a)
                a = dve(lambda k=k: V_.tensor_tensor(m2, m1, m0, ALU.mult), a)
                a = dve(lambda k=k: V_.tensor_reduce(slot_k[:, k, :], m2, AX.X, ALU.add), a)
                a = dve(lambda k=k: V_.tensor_tensor(m2, m1, W, ALU.mult), a)
                a = dve(lambda k=k: V_.tensor_reduce(w_k[:, k, :], m2, AX.X, ALU.add), a)
            a = dve(lambda: V_.tensor_scalar(w_k, w_k, 0.5, None, ALU.mult), a)
            a = dve(lambda: V_.tensor_copy(bits(idx_in), slot_k), a)
            t_idx = a

            a = dve(lambda: V_.tensor_scalar(bits(within), bits(idx_in), P - 1, None, ALU.bitwise_and), a)
            a = dve(lambda: V_.tensor_copy(within, bits(within)), a)
            a = dve(lambda: V_.tensor_tensor(slot_row, slot_k, within, ALU.subtract), a)
            a = dve(lambda: V_.tensor_scalar(kept_k, kept_k, -float(OUTSIDE), float(OUTSIDE),
                                             ALU.mult, ALU.add), a)
            a = dve(lambda: V_.scalar_tensor_tensor(out=slot_row, in0=slot_row, scalar=1.0 / P,
                                                    in1=kept_k, op0=ALU.mult, op1=ALU.add), a)
            n_all = 2 * tiles
            rows_shape = [P, n_all, SLOT_ROWS]
            hot, row_part, tile_part = (row_hot[:, :, x, :] for x in (0, 0, 1))
            a = dve(lambda: V_.tensor_tensor(
                hot, count[:, 0:SLOT_ROWS].unsqueeze(1).to_broadcast(rows_shape),
                slot_row.rearrange("p k t -> p (k t)").unsqueeze(2).to_broadcast(rows_shape),
                ALU.is_equal), a, in_consts)
            for k in range(TOP_K):
                part = slice(k * tiles, (k + 1) * tiles)
                c = dve(lambda part=part: V_.tensor_tensor(
                    tile_part[:, part, :], hot[:, part, :],
                    count[:, 0:tiles].unsqueeze(2).to_broadcast([P, tiles, SLOT_ROWS]), ALU.mult), a)
            a = dve(lambda: V_.tensor_scalar(row_part, hot, row_number, None, ALU.mult), c)
            bk = banks_m.take()
            within_flat = within.rearrange("p k t -> p (k t)")
            step_ = 16
            for j0 in range(0, n_all, step_):
                wh = within_hot.take()
                shape = [P, step_, P]
                w_ = dve(lambda wh=wh, j0=j0: V_.tensor_tensor(
                    wh.ap, count.unsqueeze(1).to_broadcast(shape),
                    within_flat[:, j0:j0 + step_].unsqueeze(2).to_broadcast(shape), ALU.is_equal),
                    a, *wh.free)
                for j in range(j0, j0 + step_):
                    p_ = pe(lambda bk=bk, wh=wh, j=j, j0=j0: T_.matmul(
                        bk.ap[:, 0:2 * SLOT_ROWS], wh.ap[:, j - j0, :],
                        row_hot[:, j, :, :].rearrange("p x r -> p (x r)"),
                        start=j == 0, stop=j == n_all - 1), w_, *bk.free, signal=j == j0 + step_ - 1)
                wh.free = (p_,)
            a = dve(lambda bk=bk: V_.tensor_copy(token_of, bk.ap[:, 0:SLOT_ROWS]), p_)
            a = dve(lambda bk=bk: V_.scalar_tensor_tensor(
                out=bits(token_of), in0=bk.ap[:, SLOT_ROWS:2 * SLOT_ROWS], scalar=float(P), in1=token_of,
                op0=ALU.mult, op1=ALU.add), a)
            bk.free = (a,)
            t_token = a

            out_slots = slots_out.rearrange("(e s p) d -> e p s d", e=EXPERTS, p=P)

            def gather_rows(e):
                i = e % 2
                for s_ in range(SLOT_TILES):
                    r = e * SLOT_TILES + s_
                    pool.transfer(lambda i=i, s_=s_, r=r: G_.indirect_dma_start(
                        rows_in[i][:, s_, :], None, tokens,
                        bass.IndirectOffsetOnAxis(ap=token_of[:, r:r + 1].bitcast(u32), axis=0),
                        bounds_check=TILES * P - 1, oob_is_err=False),
                        rows_ready[i], t_token, *(a.all for a in tokens_stored.values()), *rows_free[i])
                return rows_ready[i].all

            def turn_rows(e):
                i = e % 2
                flat_halves = halves[i].rearrange("p a b -> p (a b)")
                dT = (flat_halves[:, 0:CAP], flat_halves[:, CAP:2 * CAP])
                cps = []
                for lo_, hi_ in ((0, 4), (4, SLOT_TILES)):
                    bk = banks_m.take()
                    for s_ in range(lo_, hi_):
                        c_ = pe(lambda bk=bk, s_=s_, lo_=lo_: T_.matmul(
                            bk.ap[:, (s_ - lo_) * P:(s_ - lo_ + 1) * P], rows_in[i][:, s_, :], ident,
                            is_transpose=True), t_rows[e], *bk.free, signal=s_ == hi_ - 1)
                    cols = slice(lo_ * P, hi_ * P)
                    cp = split(dT[0][:, cols], dT[1][:, cols], bk.ap[:, 0:(hi_ - lo_) * P], c_,
                               *halves_free[i], *region_free)
                    bk.free = cp
                    cps += cp
                rows_free[i] = (c_,)
                return dT, cps

            def split_weights(e):
                i = e % 2
                gh, gl, uh, ul = (stack[i][:, 0, j, :] for j in range(4))
                t = (t_gate_up[e], *stack_free[i], *region_free)
                done = (*split(gh, gl, wg[:, i, :], *t), *split(uh, ul, wu[:, i, :], *t))
                if e + 2 < EXPERTS:
                    load_gate_up(e + 2, *done)
                return (gh, gl), (uh, ul), done

            t_rows = {e: gather_rows(e) for e in range(2)}
            halved = {0: split_weights(0)}
            turned_rows = turn_rows(0)
            for e in range(EXPERTS):
                i = wi = e % 2
                dT, cps = turned_rows
                h = hid.take()
                for f in range(HID1 // P):
                    for half in range(2):
                        cols = slice(half * HALF_CAP, (half + 1) * HALF_CAP)
                        gb, ub = bank_s.take(), bank_t.take()
                        moving = (dT[0][:, cols], dT[1][:, cols])
                        f_cols = slice(f * P, (f + 1) * P)
                        g_ = three_products(gb, gb.ap[:, 0:HALF_CAP], [w[:, f_cols] for w in halved[e][0]],
                                            moving, *cps, *halved[e][2])
                        u_ = three_products(ub, ub.ap[:, 0:HALF_CAP], [w[:, f_cols] for w in halved[e][1]],
                                            moving)
                        sg = sig.take()
                        s_ = act(lambda sg=sg, gb=gb: S_.activation(sg.ap, gb.ap[:, 0:HALF_CAP], ACT.Silu),
                                 g_, *sg.free)
                        gb.free = (s_,)
                        m_ = dve(lambda sg=sg, ub=ub, h=h, f=f, cols=cols: V_.tensor_tensor(
                            h.ap[:, f, cols], ub.ap[:, 0:HALF_CAP], sg.ap, ALU.mult), s_, u_, *h.free)
                        ub.free = (m_,)
                        sg.free = (m_,)
                        if f == 0 and half == 0 and e + 1 < EXPERTS:
                            halved[e + 1] = split_weights(e + 1)
                halves_free[i] = stack_free[i] = (u_,)
                if e + 2 < EXPERTS:
                    t_rows[e + 2] = gather_rows(e + 2)
                if e + 1 < EXPERTS:
                    turned_rows = turn_rows(e + 1)
                o = eo.take()
                outs = []
                for part, (lo_, hi_) in enumerate(((0, 4), (4, SLOT_TILES))):
                    bk = (bank_t if part else bank_o).take()
                    for s_ in range(lo_, hi_):
                        for f in range(HID1 // P):
                            d_ = pe(lambda bk=bk, s_=s_, lo_=lo_, f=f, h=h, wi=wi: T_.matmul(
                                bk.ap[:, (s_ - lo_) * P:(s_ - lo_ + 1) * P],
                                h.ap[:, f, s_ * P:(s_ + 1) * P], wd[:, wi, f, :],
                                start=f == 0, stop=f == HID1 // P - 1), m_, t_down[e], *bk.free,
                                signal=s_ == hi_ - 1 and f == HID1 // P - 1)
                    n = (hi_ - lo_) * P
                    c_ = act(lambda bk=bk, o=o, lo_=lo_, hi_=hi_, n=n: S_.activation(
                        o.ap[:, lo_:hi_, :], bk.ap[:, 0:n].rearrange("p (s d) -> p s d", d=DIM), ACT.Copy),
                        d_, *o.free)
                    bk.free = (c_,)
                h.free = (d_,)
                o.free = (sp.transfer(lambda o=o, e=e: Y_.dma_start(out_slots[e], o.ap),
                                      slots_stored[i], c_, *dram_free[0]),)
                if e + 2 < EXPERTS:
                    load_down(e + 2, d_)
            outputs_stored[0] = (slots_stored[0].all, slots_stored[1].all)
            rows_gathered[0] = (rows_ready[0].all, rows_ready[1].all)
            wqkv_free[0] = (d_, *halved[EXPERTS - 1][2])
            return (t_idx, (dve.done, dve.count), (pe.done, pe.count), (act.done, act.count),
                    (pool.done, pool.count), *outputs_stored[0])

        streams = []
        tile = 4 * SEQ
        free, at = [], 0
        if 1 in stages:
            carve = Carve(ARENA - GROUPS * SEQ)
            free = experts0(streams, 0, (carve(UP0), carve(UP0 // 2), carve(UP0 // 2)), lambda: (),
                            3 * tile, lambda: (), (N_STACK - 1, N_STACK - 2))
            at = EXPERT_ROUNDS * batches - INTO_ATTENTION
        if 2 in stages:
            free, tiles_free = attention(w_qkv0, w_out0, 4, 32, False, finish0, PIPELINE0, streams, at, free)
        if 3 in stages:
            at += batches * GROUPS + OUT_OF_ATTENTION
            n_groups = batches * GROUPS
            idle = batches * GROUPS * TILES_B % N_PROB
            memory = (wqkv[:, 0:UP0], wqkv[:, UP0:UP0 * 3 // 2], Carve((idle + 2) * tile - UP0 // 2)(UP0 // 2))
            keep_free[0] = free
            free = experts0(streams, at, memory, lambda: (*wqkv_free[0], *tiles_free(idle)),
                            idle * tile, lambda: tiles_free(idle),
                            ((n_groups - 3) % N_STACK, (n_groups - 2) % N_STACK), after=route if 4 in stages else None)
        merge(streams)
        if 4 in stages:
            free = experts1(free)
        if 5 in stages:
            streams = []
            free, _ = attention(w_qkv1, w_out1, 2, 64, True, finish1, PIPELINE1, streams, 0, list(free),
                                first=collect if 4 in stages else None, after=route if 6 in stages else None)
            merge(streams)
        if 6 in stages:
            free = experts1(free)
        if stages[-1] in (4, 6):
            for b in range(batches):
                drain(collect(b))
        stored = Arrival("stored")
        for b in range(batches):
            sp.transfer(lambda b=b: Y_.dma_start(out_v[b], X[:, b * TILES_B:(b + 1) * TILES_B, :]),
                        stored, x_ready[b])

        block = ctx.enter_context(nc.Block())

        @block.tensor
        def _(eng):
            pe.run(eng)

        @block.scalar
        def _(eng):
            act.run(eng)

        @block.vector
        def _(eng):
            dve.run(eng)

        @block.gpsimd
        def _(eng):
            pool.run(eng)

        @block.sync
        def _(eng):
            sp.run(eng)
            eng.wait_ge(stored.sem, stored.count)
            for a in (*tokens_stored.values(), *slots_stored):
                if a.count:
                    eng.wait_ge(a.sem, a.count)


def lay_out(inputs):
    f = {k: np.asarray(v) for k, v in inputs.items()}
    w1, b1 = f["L1_attn_W_qkv"], f["L1_attn_b_qkv"]
    a = {
        "x": f["L0_attn_x"],
        "w_qkv0": f["L0_attn_w_qkv"],
        "w_out0": f["L0_attn_w_out"].reshape(GROUPS, P, DIM).transpose(1, 0, 2),
        "b_out0": f["L0_attn_b_out"], "gamma0": f["L0_attn_ln_gamma"], "beta0": f["L0_attn_ln_beta"],
        "gate0": f["L0_ffn_gate_w"].T,
        "up0": f["L0_ffn_w_up"].transpose(2, 0, 1).reshape(DIM, EXPERTS * HID0),
        "down0": f["L0_ffn_w_down"].transpose(2, 0, 1).reshape(2, P, EXPERTS, DIM)
                  .transpose(1, 2, 0, 3).reshape(P, EXPERTS * 2, DIM),
        "bias0": f["L0_ffn_expert_bias"],
        "w_qkv1": w1,
        "b_qk1": b1[:2 * INNER].reshape(2 * GROUPS, P).T,
        "b_v1": b1[2 * INNER:].reshape(GROUPS, P).T,
        "w_out1": f["L1_attn_W_out"].reshape(GROUPS, P, DIM).transpose(1, 0, 2),
        "b_out1": f["L1_attn_b_out"],
        "router1": f["L1_ffn_router_w"].T,
        "wg1": f["L1_ffn_wg"].transpose(1, 0, 2),
        "wu1": f["L1_ffn_wu"].transpose(1, 0, 2),
        "wd1": f["L1_ffn_wd"].reshape(EXPERTS, HID1 // P, P, DIM).transpose(2, 0, 1, 3),
        "consts": constants(),
    }
    return {k: np.ascontiguousarray(v) for k, v in a.items()}


def kernel(**inputs):
    import concourse.bacc as _bacc
    from concourse.bass_utils import run_bass_kernel_spmd as _run

    nc = _bacc.Bacc("TRN2", target_bir_lowering=False, num_devices=1)
    arrays, args = {}, {}
    for name, a in lay_out(inputs).items():
        arrays[f"in_{name}"] = a
        args[name] = nc.dram_tensor(f"in_{name}", a.shape, mybir.dt.from_np(a.dtype),
                                    kind="ExternalInput").ap()
    out = nc.dram_tensor("out", (BATCHES, SEQ, DIM), mybir.dt.float32, kind="ExternalOutput").ap()
    build(nc, **args, out=out)
    return _run(nc, [arrays], core_ids=[0]).results[0]["out"]
```
